# Optimizing a Trainium2 kernel written in Bass

```python
import numpy as np
import jax
import jax.numpy as jnp

def _softmax(x, axis=-1):
    return jax.nn.softmax(x, axis=axis)

def _gelu(x):
    return jax.nn.gelu(x, approximate=True)

def _silu(x):
    return jax.nn.silu(x)

def _sigmoid(x):
    return jax.nn.sigmoid(x)

def _layernorm(x, axis=-1, eps=1e-05):
    m = jnp.mean(x, axis=axis, keepdims=True)
    v = jnp.var(x, axis=axis, keepdims=True)
    return (x - m) / jnp.sqrt(v + eps)

def _scatter_add(tgt, idx, src, axis=0):
    return tgt.at[idx].add(src)

def _segment_sum(src, seg, n):
    return jax.ops.segment_sum(src, seg, n)
kernel_name = 'mk_seq_preln_d1_jaxref_r8_e18716'

def setup_inputs(seed: int=0):
    np.random.seed(seed)
    _w = jnp.asarray

    def _L0_attn_setup():
        import jax, jax.numpy as jnp
        import numpy as np
        B, N, E = (4, 512, 256)
        H_DIM = 256
        HEADS = 16
        DH = H_DIM // HEADS
        LN_EPS = 1e-05

        def _heads(t):
            b, n, _ = t.shape
            return t.reshape(b, n, HEADS, DH).transpose(0, 2, 1, 3)

        def _layernorm(x, g, b):
            mu = jnp.mean(x, axis=-1, keepdims=True)
            var = jnp.mean(jnp.square(x - mu), axis=-1, keepdims=True)
            return (x - mu) * jax.lax.rsqrt(var + LN_EPS) * g + b
        key = jax.random.key(seed)
        ks = jax.random.split(key, 10)
        s = 1.0 / np.sqrt(E)
        so = 1.0 / np.sqrt(H_DIM)
        return {'x': jax.random.normal(ks[0], (B, N, E), jnp.float32), 'Wqk': jax.random.normal(ks[1], (E, H_DIM), jnp.float32) * s, 'bqk': jnp.zeros((H_DIM,), jnp.float32), 'Wv': jax.random.normal(ks[2], (E, H_DIM), jnp.float32) * s, 'bv': jnp.zeros((H_DIM,), jnp.float32), 'Wu': jax.random.normal(ks[3], (E, H_DIM), jnp.float32) * s, 'bu': jnp.zeros((H_DIM,), jnp.float32), 'Wo': jax.random.normal(ks[4], (H_DIM, E), jnp.float32) * so, 'bo': jnp.zeros((E,), jnp.float32), 'ln_g': jnp.ones((H_DIM,), jnp.float32), 'ln_b': jnp.zeros((H_DIM,), jnp.float32)}
    _L0_attn_in = _L0_attn_setup()

    def _L0_ffn_setup():
        import jax, jax.numpy as jnp
        import numpy as np
        NUM_EXPERTS = 8
        TOP_K = 2
        EMB = 256
        MLP = 512
        B, S = (4, 128)
        key = jax.random.key(seed)
        ks = jax.random.split(key, 5)
        scale_x = 1.0
        return {'x': jax.random.normal(ks[0], (B, S, EMB), dtype=jnp.float32), 'gate_kernel': jax.random.normal(ks[1], (EMB, NUM_EXPERTS), dtype=jnp.float32) / np.sqrt(EMB), 'w0_kernel': jax.random.normal(ks[2], (NUM_EXPERTS, EMB, MLP), dtype=jnp.float32) / np.sqrt(EMB), 'w1_kernel': jax.random.normal(ks[3], (NUM_EXPERTS, EMB, MLP), dtype=jnp.float32) / np.sqrt(EMB), 'wo_kernel': jax.random.normal(ks[4], (NUM_EXPERTS, MLP, EMB), dtype=jnp.float32) / np.sqrt(MLP)}
    _L0_ffn_in = _L0_ffn_setup()
    _d = {'L0_attn_x': _L0_attn_in['x'], 'L0_attn_Wqk': _L0_attn_in['Wqk'], 'L0_attn_bqk': _L0_attn_in['bqk'], 'L0_attn_Wv': _L0_attn_in['Wv'], 'L0_attn_bv': _L0_attn_in['bv'], 'L0_attn_Wu': _L0_attn_in['Wu'], 'L0_attn_bu': _L0_attn_in['bu'], 'L0_attn_Wo': _L0_attn_in['Wo'], 'L0_attn_bo': _L0_attn_in['bo'], 'L0_attn_ln_g': _L0_attn_in['ln_g'], 'L0_attn_ln_b': _L0_attn_in['ln_b'], 'L0_ffn_gate_kernel': _L0_ffn_in['gate_kernel'], 'L0_ffn_w0_kernel': _L0_ffn_in['w0_kernel'], 'L0_ffn_w1_kernel': _L0_ffn_in['w1_kernel'], 'L0_ffn_wo_kernel': _L0_ffn_in['wo_kernel']}
    _x0 = _d['L0_attn_x']
    _d['L0_attn_x'] = jax.random.normal(jax.random.fold_in(jax.random.key(seed), 1), (4, 512, 256), dtype=_x0.dtype)
    del _x0
    return _d

def reference(L0_attn_x, L0_attn_Wqk, L0_attn_bqk, L0_attn_Wv, L0_attn_bv, L0_attn_Wu, L0_attn_bu, L0_attn_Wo, L0_attn_bo, L0_attn_ln_g, L0_attn_ln_b, L0_ffn_gate_kernel, L0_ffn_w0_kernel, L0_ffn_w1_kernel, L0_ffn_wo_kernel):

    def _L0_attn_ref(x, Wqk, bqk, Wv, bv, Wu, bu, Wo, bo, ln_g, ln_b):
        import jax, jax.numpy as jnp
        import numpy as np
        B, N, E = (4, 512, 256)
        H_DIM = 256
        HEADS = 16
        DH = H_DIM // HEADS
        LN_EPS = 1e-05

        def _heads(t):
            b, n, _ = t.shape
            return t.reshape(b, n, HEADS, DH).transpose(0, 2, 1, 3)

        def _layernorm(x, g, b):
            mu = jnp.mean(x, axis=-1, keepdims=True)
            var = jnp.mean(jnp.square(x - mu), axis=-1, keepdims=True)
            return (x - mu) * jax.lax.rsqrt(var + LN_EPS) * g + b
        q = x @ Wqk + bqk
        k = x @ Wqk + bqk
        v = jax.nn.silu(x @ Wv + bv)
        u = jax.nn.silu(x @ Wu + bu)
        q = jax.nn.elu(_heads(q))
        kh = jax.nn.elu(_heads(k))
        vh = _heads(v)
        kv = jnp.einsum('bhnd,bhne->bhde', kh, vh)
        out = jnp.einsum('bhnd,bhde->bhne', q, kv)
        out = out.transpose(0, 2, 1, 3).reshape(x.shape[0], x.shape[1], H_DIM)
        out = _layernorm(out, ln_g, ln_b)
        out = u * out
        return out @ Wo + bo

    def _L0_ffn_ref(x, gate_kernel, w0_kernel, w1_kernel, wo_kernel):
        import jax, jax.numpy as jnp
        import numpy as np
        NUM_EXPERTS = 8
        TOP_K = 2
        EMB = 256
        MLP = 512
        B, S = (4, 128)
        gate_logits = jnp.einsum('bsd,de->bse', x, gate_kernel)
        top_k_weights, top_k_indices = jax.lax.top_k(gate_logits, TOP_K)
        top_k_weights = jax.nn.softmax(top_k_weights.astype(jnp.float32), axis=-1).astype(x.dtype)
        one_hot = jax.nn.one_hot(top_k_indices, NUM_EXPERTS, dtype=x.dtype)
        combine = jnp.einsum('bsk,bske->bse', top_k_weights, one_hot)
        h0 = jnp.einsum('bsd,edm->bsem', x, w0_kernel)
        h1 = jnp.einsum('bsd,edm->bsem', x, w1_kernel)
        inter = jax.nn.silu(h0) * h1
        out = jnp.einsum('bse,bsem,emd->bsd', combine, inter, wo_kernel)
        return out
    x = L0_attn_x
    x = x + _L0_attn_ref(_layernorm(x, axis=-1), L0_attn_Wqk, L0_attn_bqk, L0_attn_Wv, L0_attn_bv, L0_attn_Wu, L0_attn_bu, L0_attn_Wo, L0_attn_bo, L0_attn_ln_g, L0_attn_ln_b)
    x = x + _L0_ffn_ref(_layernorm(x, axis=-1), L0_ffn_gate_kernel, L0_ffn_w0_kernel, L0_ffn_w1_kernel, L0_ffn_wo_kernel)
    return x

_drawn_inputs = setup_inputs


def setup_inputs(seed=0):
    import zlib

    import numpy as np

    out = dict(_drawn_inputs(seed))
    spreads = {'L0_attn_bqk': (0.0, 0.1),
     'L0_attn_bv': (0.0, 0.1),
     'L0_attn_bu': (0.0, 0.1),
     'L0_attn_bo': (0.0, 0.1),
     'L0_attn_ln_g': (1.0, 0.2),
     'L0_attn_ln_b': (0.0, 0.1)}
    factors = {}
    for name, (base, spread) in spreads.items():
        noise = np.random.default_rng([zlib.crc32(name.encode()), seed]).standard_normal(out[name].shape)
        drawn = base * np.exp(spread * noise) if base else spread * noise
        out[name] = jnp.asarray(drawn.astype(out[name].dtype))
    for name, factor in factors.items():
        out[name] = (out[name] * factor).astype(out[name].dtype)
    return out
```

```python
import concourse.bass as bass
from concourse import mybir
from contextlib import ExitStack


def linear_attention_then_top2_moe(nc, x, Wqk, bqk, Wv, bv, Wu, bu, Wo, bo, ln_g, ln_b, gate, w0, w1, wo, out):
    f32, f16, bf16, i32 = mybir.dt.float32, mybir.dt.float16, mybir.dt.bfloat16, mybir.dt.int32
    ALU, ACT, AX = mybir.AluOpType, mybir.ActivationFunctionType, mybir.AxisListType

    P = 128
    T, E = x.shape
    EXPERTS, _, MLP = w0.shape
    TILES = T // P
    PER = 4
    GROUPS = TILES // PER
    DH = 16
    KT = E // P
    MT = MLP // P
    EPS = 1e-5
    TOP = 2
    REGION = T + P
    SPARE = EXPERTS * REGION
    BLOCKS = (TOP * T + EXPERTS * (P - 1)) // P
    XW, WW, IW = 256.0, 256.0, 64.0

    HI, LO, COMB, TOK, ROW = 0, E // 2, E, E + EXPERTS, E + 16
    CH = 1024
    NCH = 3
    EW = NCH * CH

    sent = nc.dram_tensor("sent", (SPARE + P, ROW), f32).ap()

    ctx = ExitStack()
    with ctx:
        def sb(name, shape, dt):
            return ctx.enter_context(nc.sbuf_tensor(name, shape, dt))

        def pb(name, shape, dt):
            return ctx.enter_context(nc.psum_tensor(name, shape, dt))

        def sem(name):
            return ctx.enter_context(nc.semaphore(name))

        ident = sb("ident", [P, P], f32)
        ident16 = sb("ident16", [P, P], f16)
        before = sb("before", [P, P], bf16)
        ones16 = sb("ones16", [P, P], bf16)
        headmask = sb("headmask", [P, KT * P], f32)
        neghalf = sb("neghalf", [P, TILES], f32)
        desc = sb("desc", [P, PER, EXPERTS], f32)
        region0 = sb("region0", [P, PER, EXPERTS], f32)
        thresholds = sb("thresholds", [P, EXPERTS, TILES], f32)
        blockno = sb("blockno", [P, BLOCKS, EXPERTS], f32)
        block128 = sb("block128", [P, BLOCKS], f32)
        oneE = sb("oneE", [P, EXPERTS], f32)
        tokno = sb("tokno", [P, TILES], i32)
        padrows = sb("padrows", [P, ROW], f32)
        gamma = sb("gamma", [P, E], f32)
        beta = sb("beta", [P, E], f32)
        wcat = sb("wcat", [P, KT, 3 * E], f32)
        wout = sb("wout", [P, KT, E], f32)
        gatew = sb("gatew", [P, KT, EXPERTS], f32)
        bias3 = sb("bias3", [3, 4 * E], bf16)
        stage = sb("stage", [P, NCH, CH], f32)
        w_hi = sb("w_hi", [P, EXPERTS, EW], f16)
        w_lo = sb("w_lo", [P, EXPERTS, EW], f16)
        xall = sb("xall", [P, TILES, E], f32)
        vuall = sb("vuall", [P, TILES, 2 * E], f32)
        brow = vuall[0:1, TILES - 2:TILES, :].rearrange("p t n -> p (t n)")
        brest = vuall[0:1, TILES - 4:TILES - 2, :].rearrange("p t n -> p (t n)")
        bpart = vuall[0:1, TILES - 7:TILES - 4, :].rearrange("p t n -> p (t n)").bitcast(bf16)\
            .rearrange("p (b n) -> p b n", b=3)
        st1 = sb("st1", [P, TILES, 6], f32)
        mv1 = sb("mv1", [P, TILES, 2], f32)
        ve1 = sb("ve1", [P, TILES], f32)
        rs1 = sb("rs1", [P, TILES], f32)
        xn = sb("xn", [P, 2, E], f32)
        xT = sb("xT", [P, 2, KT, P], f32)
        eq = sb("eq", [P, 2, E], f32)
        q = sb("q", [P, 2, E], f32)
        qT = sb("qT", [P, PER, KT, P], f32)
        kv = sb("kv", [P, KT * P], f32)
        st2 = sb("st2", [P, PER, 6], f32)
        mv2 = sb("mv2", [P, PER, 2], f32)
        ve2 = sb("ve2", [P, PER], f32)
        rs2 = sb("rs2", [P, PER], f32)
        on = sb("on", [P, 2, E], f32)
        y = on
        yT = sb("yT", [P, KT, P], f32)
        x2 = sb("x2", [P, PER, E], f32)
        st3 = sb("st3", [P, PER, 6], f32)
        mv3 = sb("mv3", [P, PER, 2], f32)
        ve3 = sb("ve3", [P, PER], f32)
        rs3 = sb("rs3", [P, PER], f32)
        z = sb("z", [P, 2, E], f32)
        zT = sb("zT", [P, KT, P], f32)
        rows = sb("rows", [P, PER, ROW], f32)
        lg = sb("lg", [P, PER, EXPERTS], f32)
        lg2 = sb("lg2", [P, PER, EXPERTS], f32)
        same = sb("same", [P, PER, EXPERTS], f32)
        first = sb("first", [P, PER, EXPERTS], f32)
        oh0 = sb("oh0", [P, PER, EXPERTS], f32)
        oh1 = sb("oh1", [P, PER, EXPERTS], f32)
        c0 = sb("c0", [P, PER, EXPERTS], f32)
        c1 = sb("c1", [P, PER, EXPERTS], f32)
        chosen = sb("chosen", [P, PER, EXPERTS], bf16)
        sofar = sb("sofar", [P, PER + 1, EXPERTS], bf16)
        m0 = sb("m0", [P, PER], f32)
        m1 = sb("m1", [P, PER], f32)
        k0 = sb("k0", [P, PER], f32)
        dm = sb("dm", [P, PER], f32)
        ex = sb("ex", [P, PER], f32)
        p0 = sb("p0", [P, PER], f32)
        p1 = sb("p1", [P, PER], f32)
        place = sb("place", [P, PER, EXPERTS], f32)
        slots = sb("slots", [P, TOP, PER], f32)
        slots_i = sb("slots_i", [P, TOP, PER], i32)
        count = sb("count", [P, EXPERTS], f32)
        nblk = sb("nblk", [P, EXPERTS], f32)
        ends = sb("ends", [P, EXPERTS], f32)
        padoff = sb("padoff", [P, EXPERTS], f32)
        bexp_i = sb("bexp_i", [P, BLOCKS], i32)
        boff_i = sb("boff_i", [P, BLOCKS], i32)
        padoff_i = sb("padoff_i", [P, EXPERTS], i32)
        room = vuall[:, :, :].rearrange("p t n -> p (t n)")
        at = [0]

        def cut(words):
            at[0] += words
            return room[:, at[0] - words:at[0]]
        SL = 4
        blk = [cut(ROW) for _ in range(SL)]
        sil = [cut(MLP) for _ in range(2)]
        inter = [cut(MLP) for _ in range(2)]
        xb = [cut(2 * KT * P // 2).bitcast(f16).rearrange("p (k t) -> p k t", t=P) for _ in range(2)]
        ih = [cut(MLP // 2).bitcast(f16).rearrange("p (k t) -> p k t", t=P) for _ in range(2)]
        il = [cut(MLP // 2).bitcast(f16).rearrange("p (k t) -> p k t", t=P) for _ in range(2)]
        ys = [cut(E) for _ in range(SL)]
        over = cut(EXPERTS * TILES).rearrange("p (e t) -> p e t", t=TILES)
        past = cut(BLOCKS * EXPERTS).rearrange("p (j e) -> p j e", e=EXPERTS)
        past2 = cut(BLOCKS * EXPERTS).rearrange("p (j e) -> p j e", e=EXPERTS)
        bexp = cut(BLOCKS)
        bstart = cut(BLOCKS)
        boff = cut(BLOCKS)
        assert at[0] <= TILES * 2 * E

        bank = [pb(f"bank{n}", [P, 512], f32) for n in range(8)]
        pVU = [bank[0][:, :], bank[1][:, :]]
        pQ = [bank[2][:, 0:E], bank[3][:, 0:E]]
        pXT = [bank[2][:, E:2 * E], bank[3][:, E:2 * E]]
        pKV = bank[4][:, 0:KT * P]
        pQT = bank[5][:, 0:E]
        pO = bank[5][:, E:2 * E]
        pYT = bank[6][:, 0:E]
        pW = bank[6][:, E:2 * E]
        pZT = bank[7][:, 0:E]
        pG = bank[7][:, E:E + EXPERTS]
        pR = bank[7][:, 320:320 + PER * EXPERTS]
        pC = bank[4][:, 384:384 + EXPERTS]
        pH0 = [bank[0][:, :], bank[2][:, :]]
        pH1 = [bank[1][:, :], bank[3][:, :]]
        pXB = bank[4][:, 0:KT * P].bitcast(f16).rearrange("p (k t) -> p k t", t=P)
        pIT = bank[5][:, :]
        pY = [bank[6][:, 0:E], bank[7][:, 0:E]]

        s_const = sem("s_const")
        s_xin = [sem(f"s_xin{g}") for g in range(GROUPS)]
        s_wA = sem("s_wA")
        s_brow = sem("s_brow")
        s_bsplit = sem("s_bsplit")
        s_bias3 = sem("s_bias3")
        s_gb = sem("s_gb")
        s_gbh = sem("s_gbh")
        s_stage = [sem(f"s_stage{n}") for n in range(NCH)]
        s_whi = sem("s_whi")
        s_wlo = sem("s_wlo")
        s_st1 = sem("s_st1")
        s_mv1 = sem("s_mv1")
        s_ve1 = sem("s_ve1")
        s_rs1 = sem("s_rs1")
        s_xn = sem("s_xn")
        s_XT = sem("s_XT")
        s_xT = sem("s_xT")
        s_Q = sem("s_Q")
        s_VU = sem("s_VU")
        s_exp = sem("s_exp")
        s_tanh = sem("s_tanh")
        s_em1 = sem("s_em1")
        s_q = sem("s_q")
        s_vu = sem("s_vu")
        s_KV = sem("s_KV")
        s_QT = sem("s_QT")
        s_qT = sem("s_qT")
        s_kv = sem("s_kv")
        s_O = sem("s_O")
        s_st2 = sem("s_st2")
        s_mv2 = sem("s_mv2")
        s_ve2 = sem("s_ve2")
        s_rs2 = sem("s_rs2")
        s_on = sem("s_on")
        s_ong = sem("s_ong")
        s_onb = sem("s_onb")
        s_y = sem("s_y")
        s_YT = sem("s_YT")
        s_yT = sem("s_yT")
        s_W = sem("s_W")
        s_x2 = sem("s_x2")
        s_st3 = sem("s_st3")
        s_mv3 = sem("s_mv3")
        s_ve3 = sem("s_ve3")
        s_rs3 = sem("s_rs3")
        s_z = sem("s_z")
        s_hi = sem("s_hi")
        s_lo = sem("s_lo")
        s_ZT = sem("s_ZT")
        s_zT = sem("s_zT")
        s_G = sem("s_G")
        s_lg = sem("s_lg")
        s_route = sem("s_route")
        s_dm = sem("s_dm")
        s_ex = sem("s_ex")
        s_chosen = sem("s_chosen")
        s_R = sem("s_R")
        s_slots = sem("s_slots")
        s_rowsfree = sem("s_rowsfree")
        s_sent = sem("s_sent")
        s_store = sem("s_store")
        s_x2free = sem("s_x2free")
        s_spare = sem("s_spare")
        s_C = sem("s_C")
        s_table = sem("s_table")
        s_padA = sem("s_padA")
        s_padS = sem("s_padS")
        s_blk = [sem(f"s_blk{n}") for n in range(SL)]
        s_XB = sem("s_XB")
        s_xb = sem("s_xb")
        s_H0 = sem("s_H0")
        s_H1 = sem("s_H1")
        s_sil = sem("s_sil")
        s_inter = sem("s_inter")
        s_IT = sem("s_IT")
        s_ih = sem("s_ih")
        s_il = sem("s_il")
        s_Y = sem("s_Y")
        s_ys = sem("s_ys")
        s_added = sem("s_added")

        block = ctx.enter_context(nc.Block())

        CONST_STEPS = 19
        FIRST = EXPERTS - GROUPS
        ROUTE = 24

        def tile_of(buf, i):
            return buf[:, bass.ds(i, 1), :].rearrange("p a n -> p (a n)")

        def weights_of(part, e, c0_, n):
            return part[:, bass.ds(e, 1), c0_:c0_ + n].rearrange("p a n -> p (a n)")

        def chunk_source(e, c):
            if c < 2:
                return (w0, w1)[c][bass.ds(e, 1), :, :].rearrange("a (k p) n -> p (a k) n", p=P)
            return wo[bass.ds(e, 1), :, :].rearrange("a (k p) n -> p (a k) n", p=P)

        def chunk_view(c):
            w = MLP if c < 2 else E
            return stage[:, c, :].rearrange("p (k n) -> p k n", n=w)

        def chunk_in_step(s, c):
            return NCH * (FIRST + s - 1) + c

        @block.sync
        def _(sp):
            sp.sem_inc(s_x2free, 1)
            for g in range(GROUPS):
                sp.dma_start(xall[:, PER * g:PER * g + PER, :],
                             x[P * PER * g:P * PER * (g + 1), :].rearrange("(t p) e -> p t e", p=P)).then_inc(s_xin[g], 16)
                if g == 0:
                    sp.dma_start(brow[:, 0:E], bqk.rearrange("(a n) -> a n", a=1)).then_inc(s_brow, 16)
                    sp.dma_start(brow[:, E:2 * E], bv.rearrange("(a n) -> a n", a=1)).then_inc(s_brow, 16)
                    sp.dma_start(brow[:, 2 * E:3 * E], bu.rearrange("(a n) -> a n", a=1)).then_inc(s_brow, 16)
                    sp.dma_start(brow[:, 3 * E:4 * E], bo.rearrange("(a n) -> a n", a=1)).then_inc(s_brow, 16)
            for n in range(NCH):
                sp.dma_start(chunk_view(n), chunk_source(0, n)).then_inc(s_stage[n], 16)
            sp.wait_ge(s_bsplit, 5)
            for n in range(3):
                sp.dma_start(bias3[n:n + 1, :], bpart[:, n, :]).then_inc(s_bias3, 16)
            for n in range(NCH, FIRST * NCH):
                sp.wait_ge(s_wlo, n - NCH + 1)
                sp.dma_start(chunk_view(n % NCH), chunk_source(n // NCH, n % NCH)).then_inc(s_stage[n % NCH], 16)
            sp.wait_ge(s_const, CONST_STEPS)
            sp.dma_start(sent[SPARE:SPARE + P, :], padrows[:, :]).then_inc(s_spare, 16)
            sp.dma_start(out[T:T + P, :], padrows[:, 0:E]).then_inc(s_spare, 16)

            def stores(s):
                for c in range(NCH):
                    sp.wait_ge(s_wlo, chunk_in_step(s, c) - 2)
                    sp.dma_start(chunk_view(c), chunk_source(FIRST - 1 + s, c)).then_inc(s_stage[c], 16)
                for t in range(PER):
                    i = PER * (s - 1) + t
                    sp.wait_ge(s_x2, i + 1)
                    sp.dma_start(out[bass.ds(i * P, P), :], x2[:, t, :]).then_inc(s_store, 16)
                sp.wait_ge(s_store, 16 * PER * s)
                sp.sem_inc(s_x2free, 1)
            with sp.Fori(1, GROUPS + 1) as s:
                stores(s)
            sp.wait_ge(s_table, 1)
            for e in range(EXPERTS // 2, EXPERTS):
                off = sp.value_load(padoff_i[0:1, e:e + 1], min_val=0, max_val=SPARE - P)
                sp.dma_start(sent[bass.ds(off, P), :], padrows[:, :]).then_inc(s_padS, 16)
            sp.wait_ge(s_padS, 16 * (EXPERTS // 2))
            sp.wait_ge(s_padA, 16 * (EXPERTS // 2))
            sp.wait_ge(s_spare, 32)
            sp.wait_ge(s_sent, 16 * TOP * TILES)

            def load(j, slot):
                off = sp.value_load(boff_i[0:1, bass.ds(j, 1)], min_val=0, max_val=SPARE)
                sp.dma_start(blk[slot], sent[bass.ds(off, P), :]).then_inc(s_blk[slot], 16)
            for j in range(SL):
                load(j, j)
            with sp.Fori(0, (BLOCKS - SL) // SL) as k:
                for r in range(SL):
                    sp.wait_ge(s_added, 16 * (SL * k + r + 1))
                    load(SL * k + SL + r, r)
            for j in range(BLOCKS - (BLOCKS - SL) % SL, BLOCKS):
                sp.wait_ge(s_added, 16 * (j - SL + 1))
                load(j, j % SL)
            sp.wait_ge(s_added, 16 * BLOCKS)

        @block.gpsimd
        def _(pool):
            g = nc.gpsimd
            pool.sem_inc(s_rowsfree, 1)
            g.memset(ident[:], 0.0).then_inc(s_const, 1)
            g.memset(ident16[:], 0.0).then_inc(s_const, 1)
            g.memset(before[:], 1.0).then_inc(s_const, 1)
            g.memset(headmask[:], 0.5).then_inc(s_const, 1)
            g.memset(neghalf[:], -0.5).then_inc(s_const, 1)
            pool.wait_ge(s_const, 5)
            g.affine_select(out=ident[:], in_=ident[:], compare_op=ALU.not_equal, fill=1.0, base=0,
                            pattern=[[-1, P]], channel_multiplier=1).then_inc(s_const, 1)
            g.affine_select(out=ident16[:], in_=ident16[:], compare_op=ALU.not_equal, fill=1.0, base=0,
                            pattern=[[-1, P]], channel_multiplier=1).then_inc(s_const, 1)
            g.affine_select(out=before[:], in_=before[:], compare_op=ALU.is_gt, fill=0.0, base=0,
                            pattern=[[1, P]], channel_multiplier=-1).then_inc(s_const, 1)
            hm = headmask[:].rearrange("p (k a c) -> p k a c", k=KT, c=DH)
            g.affine_select(out=hm, in_=hm, compare_op=ALU.is_ge, fill=0.0, base=0,
                            pattern=[[0, KT], [-DH, P // DH], [0, DH]], channel_multiplier=1).then_inc(s_const, 1)
            pool.wait_ge(s_ve1, 1)
            g.tensor_tensor(rs1[:, 0:PER], ve1[:, 0:PER], neghalf[:, 0:PER], ALU.pow).then_inc(s_rs1, 1)
            pool.wait_ge(s_const, 9)
            g.affine_select(out=hm, in_=hm, compare_op=ALU.is_ge, fill=0.0, base=DH - 1,
                            pattern=[[0, KT], [DH, P // DH], [0, DH]], channel_multiplier=-1).then_inc(s_const, 1)
            g.iota(desc[:], [[0, PER], [-1, EXPERTS]], base=EXPERTS, channel_multiplier=0,
                   allow_small_or_imprecise_dtypes=True).then_inc(s_const, 1)
            g.iota(region0[:], [[0, PER], [REGION, EXPERTS]], base=0, channel_multiplier=0,
                   allow_small_or_imprecise_dtypes=True).then_inc(s_const, 1)
            g.iota(thresholds[:], [[0, EXPERTS], [P, TILES]], base=0, channel_multiplier=0,
                   allow_small_or_imprecise_dtypes=True).then_inc(s_const, 1)
            g.iota(blockno[:], [[1, BLOCKS], [0, EXPERTS]], base=0, channel_multiplier=0,
                   allow_small_or_imprecise_dtypes=True).then_inc(s_const, 1)
            g.iota(block128[:], [[P, BLOCKS]], base=0, channel_multiplier=0,
                   allow_small_or_imprecise_dtypes=True).then_inc(s_const, 1)
            g.iota(tokno[:], [[P, TILES]], base=0, channel_multiplier=1).then_inc(s_const, 1)
            g.memset(padrows[:], 0.0).then_inc(s_const, 1)
            pool.wait_ge(s_const, 17)
            g.iota(padrows[:, TOK:TOK + 1].bitcast(i32), [[0, 1]], base=T, channel_multiplier=1).then_inc(s_const, 1)
            g.memset(rows[:], 0.0).then_inc(s_const, 1)
            for grp in range(1, GROUPS):
                pool.wait_ge(s_ve1, grp + 1)
                g.tensor_tensor(rs1[:, PER * grp:PER * grp + PER], ve1[:, PER * grp:PER * grp + PER],
                                neghalf[:, 0:PER], ALU.pow).then_inc(s_rs1, 1)
            pool.wait_ge(s_gbh, 2)

            def steps(s):
                for t in range(PER + 1):
                    i = PER * (s - 1) + t
                    if t < PER:
                        pool.wait_ge(s_ve2, i + 1)
                        g.tensor_tensor(rs2[:, t:t + 1], ve2[:, t:t + 1], neghalf[:, 0:1], ALU.pow).then_inc(s_rs2, 1)
                        pool.wait_ge(s_on, i + 1)
                        g.tensor_tensor(on[:, t % 2, :], on[:, t % 2, :], gamma[:], ALU.mult).then_inc(s_ong, 1)
                        pool.wait_ge(s_ong, i + 1)
                        g.tensor_tensor(on[:, t % 2, :], on[:, t % 2, :], beta[:], ALU.add).then_inc(s_onb, 1)
                    if t >= 1:
                        pool.wait_ge(s_ve3, i)
                        g.tensor_tensor(rs3[:, t - 1:t], ve3[:, t - 1:t], neghalf[:, 0:1], ALU.pow).then_inc(s_rs3, 1)
                pool.wait_ge(s_slots, s)
                pool.nop(nofuse=True)
                for t in range(PER):
                    for k in range(TOP):
                        g.indirect_dma_start(sent, bass.IndirectOffsetOnAxis(slots_i[:, k, t:t + 1], 0),
                                             rows[:, t, :], None).then_inc(s_sent, 16)
                pool.wait_ge(s_sent, 16 * TOP * PER * s)
                pool.sem_inc(s_rowsfree, 1)
            with pool.Fori(1, GROUPS + 1) as s:
                steps(s)

            pool.wait_ge(s_store, 16 * TILES)
            pool.wait_ge(s_spare, 32)

            def add_block(j, slot, head):
                pool.wait_ge(s_ys, j + 1)
                if not head:
                    pool.wait_ge(s_added, 16 * j)
                pool.nop(nofuse=True)
                g.indirect_dma_start(out, bass.IndirectOffsetOnAxis(blk[slot][:, TOK:TOK + 1].bitcast(i32), 0),
                                     ys[slot], None, compute_op=ALU.add).then_inc(s_added, 16)
            add_block(0, 0, True)
            with pool.Fori(0, (BLOCKS - 3) // SL) as k:
                for r in range(SL):
                    add_block(SL * k + 1 + r, (1 + r) % SL, False)
            for j in range(BLOCKS - 2, BLOCKS):
                add_block(j, j % SL, False)

        @block.scalar
        def _(act):
            a = nc.scalar
            for src, lo_ in ((Wqk, 0), (Wv, E), (Wu, 2 * E)):
                act.dma_start(wcat[:, :, lo_:lo_ + E], src.rearrange("(k p) n -> p k n", p=P)).then_inc(s_wA, 16)
            act.dma_start(wout[:], Wo.rearrange("(k p) n -> p k n", p=P)).then_inc(s_wA, 16)
            act.dma_start(gatew[:], gate.rearrange("(k p) n -> p k n", p=P)).then_inc(s_wA, 16)
            act.dma_start(gamma[:], ln_g.rearrange("(a n) -> a n", a=1).broadcast_to([P, E])).then_inc(s_gb, 16)
            act.dma_start(beta[:], ln_b.rearrange("(a n) -> a n", a=1).broadcast_to([P, E])).then_inc(s_gb, 16)

            def chunk_high(e, c):
                act.wait_ge(s_stage[c], 16 * (e + 1))
                a.activation(weights_of(w_hi, e, c * CH, CH), stage[:, c, :], ACT.Copy, scale=WW).then_inc(s_whi, 1)

            def steps(s, one, two):
                for t in range(PER + 2 if two else PER):
                    i1, i2 = PER * s + t, PER * (s - 1) + t
                    if one and t < PER:
                        act.wait_ge(s_XT, i1 + 1)
                        a.activation(xT[:, t % 2, :, :].rearrange("p k t -> p (k t)"), pXT[t % 2], ACT.Copy).then_inc(s_xT, 1)
                    if two and t >= 2:
                        if t == 2:
                            act.wait_ge(s_rowsfree, s)
                        act.wait_ge(s_z, i2 - 1)
                        a.activation(rows[:, t - 2, HI:HI + E // 2].bitcast(f16), z[:, t % 2, :], ACT.Copy, scale=XW)\
                         .then_inc(s_hi, 1)
                    if two and 1 <= t <= PER:
                        act.wait_ge(s_YT, i2)
                        a.activation(yT[:].rearrange("p k t -> p (k t)"), pYT, ACT.Copy).then_inc(s_yT, 1)
                    if one and t < PER:
                        act.wait_ge(s_Q, i1 + 1)
                        a.activation(eq[:, t % 2, :], pQ[t % 2], ACT.Exp).then_inc(s_exp, 1)
                        act.wait_ge(s_VU, i1 + 1)
                        a.activation(tile_of(vuall, i1), pVU[t % 2], ACT.Tanh, scale=0.5).then_inc(s_tanh, 1)
                    if two and t < NCH:
                        chunk_high(FIRST - 1 + s, t)
                    if one and not two:
                        for n in range(FIRST * NCH * t // PER, FIRST * NCH * (t + 1) // PER):
                            chunk_high(n // NCH, n % NCH)
                    if two and t >= 2:
                        act.wait_ge(s_ZT, i2 - 1)
                        a.activation(zT[:].rearrange("p k t -> p (k t)"), pZT, ACT.Copy).then_inc(s_zT, 1)
                    if one and t < PER:
                        act.wait_ge(s_QT, i1 + 1)
                        a.activation(qT[:, t, :, :].rearrange("p k t -> p (k t)"), pQT, ACT.Copy).then_inc(s_qT, 1)
                if two:
                    act.wait_ge(s_dm, s)
                    a.activation(ex[:], dm[:], ACT.Exp).then_inc(s_ex, 1)
            steps(0, True, False)
            with act.Fori(1, GROUPS) as s:
                steps(s, True, True)
            steps(GROUPS, False, True)

            act.wait_ge(s_table, 1)
            for e in range(EXPERTS // 2):
                off = act.value_load(padoff_i[0:1, e:e + 1], min_val=0, max_val=SPARE - P)
                act.dma_start(sent[bass.ds(off, P), :], padrows[:, :]).then_inc(s_padA, 16)

            def step(j, par):
                act.wait_ge(s_H0, j + 1)
                a.activation(sil[par], pH0[par], ACT.Silu, scale=1.0 / (XW * WW)).then_inc(s_sil, 1)
                act.wait_ge(s_IT, j + 1)
                a.activation(ih[par].rearrange("p k t -> p (k t)"), pIT, ACT.Copy).then_inc(s_ih, 1)
            step(0, 0)
            with act.Fori(0, (BLOCKS - 3) // SL) as k:
                for r in range(SL):
                    step(SL * k + 1 + r, (1 + r) % 2)
            for j in range(BLOCKS - 2, BLOCKS):
                step(j, j % 2)

        @block.vector
        def _(dve):
            v = nc.vector

            def ln1_stats(grp):
                dve.wait_ge(s_xin[grp], 16)
                for i in range(PER * grp, PER * grp + PER):
                    v.bn_stats(st1[:, i, :], xall[:, i, :]).then_inc(s_st1, 1)
                for i in range(PER * grp, PER * grp + PER):
                    dve.wait_ge(s_st1, i + 1)
                    v.bn_aggr(mv1[:, i, :], st1[:, i, :]).then_inc(s_mv1, 1)
                dve.wait_ge(s_mv1, PER * grp + PER)
                v.tensor_scalar(ve1[:, PER * grp:PER * grp + PER], mv1[:, PER * grp:PER * grp + PER, 1], EPS, None,
                                ALU.add).then_inc(s_ve1, 1)
            ln1_stats(0)
            dve.wait_ge(s_brow, 64)
            v.tensor_copy(bpart[:, 0, :], brow).then_inc(s_bsplit, 1)
            dve.wait_ge(s_bsplit, 1)
            v.tensor_tensor(brest, brow, bpart[:, 0, :], ALU.subtract).then_inc(s_bsplit, 1)
            dve.wait_ge(s_bsplit, 2)
            v.tensor_copy(bpart[:, 1, :], brest).then_inc(s_bsplit, 1)
            dve.wait_ge(s_bsplit, 3)
            v.tensor_tensor(brow, brest, bpart[:, 1, :], ALU.subtract).then_inc(s_bsplit, 1)
            dve.wait_ge(s_bsplit, 4)
            v.tensor_copy(bpart[:, 2, :], brow).then_inc(s_bsplit, 1)
            dve.wait_ge(s_gb, 32)
            v.tensor_scalar(gamma[:], gamma[:], 0.5, None, ALU.mult).then_inc(s_gbh, 1)
            v.tensor_scalar(beta[:], beta[:], 0.5, None, ALU.mult).then_inc(s_gbh, 1)
            v.memset(sofar[:], 0.0).then_inc(s_gbh, 1)
            v.memset(ones16[:], 1.0).then_inc(s_gbh, 1)
            v.memset(oneE[:], 1.0).then_inc(s_gbh, 1)
            dve.wait_ge(s_const, CONST_STEPS)
            dve.wait_ge(s_gbh, 5)

            def chunk_low(e, c):
                dve.wait_ge(s_whi, NCH * e + c + 1)
                v.scalar_tensor_tensor(weights_of(w_lo, e, c * CH, CH), stage[:, c, :], WW,
                                       weights_of(w_hi, e, c * CH, CH), ALU.mult, ALU.subtract).then_inc(s_wlo, 1)

            def route(s):
                base = [ROUTE * (s - 1)]

                def link(ins):
                    base[0] = base[0] + 1
                    ins.then_inc(s_route, 1)
                    dve.wait_ge(s_route, base[0])

                def wide(small):
                    return small.unsqueeze(2).to_broadcast([P, PER, EXPERTS])
                dve.wait_ge(s_lg, PER * s)
                link(v.tensor_reduce(m0[:], lg[:], AX.X, ALU.max))
                link(v.tensor_tensor(same[:], lg[:], wide(m0[:]), ALU.is_equal))
                link(v.tensor_tensor(first[:], same[:], desc[:], ALU.mult))
                link(v.tensor_reduce(k0[:], first[:], AX.X, ALU.max))
                link(v.tensor_tensor(oh0[:], first[:], wide(k0[:]), ALU.is_equal))
                link(v.scalar_tensor_tensor(lg2[:], oh0[:], -3.0e38, lg[:], ALU.mult, ALU.add))
                link(v.tensor_reduce(m1[:], lg2[:], AX.X, ALU.max))
                v.tensor_tensor(dm[:], m1[:], m0[:], ALU.subtract).then_inc(s_dm, 1)
                link(v.tensor_tensor(same[:], lg2[:], wide(m1[:]), ALU.is_equal))
                link(v.tensor_tensor(first[:], same[:], desc[:], ALU.mult))
                link(v.tensor_reduce(k0[:], first[:], AX.X, ALU.max))
                link(v.tensor_tensor(oh1[:], first[:], wide(k0[:]), ALU.is_equal))
                link(v.tensor_copy(sofar[:, 0, :], sofar[:, PER, :]))
                link(v.tensor_tensor(chosen[:], oh0[:], oh1[:], ALU.add))
                for t in range(PER):
                    link(v.tensor_tensor(sofar[:, t + 1, :], sofar[:, t, :], chosen[:, t, :], ALU.add))
                dve.sem_inc(s_chosen, 1)
                dve.wait_ge(s_ex, s)
                link(v.tensor_scalar(dm[:], ex[:], 1.0, None, ALU.add))
                link(v.reciprocal(p0[:], dm[:]))
                link(v.tensor_tensor(p1[:], ex[:], p0[:], ALU.mult))
                v.tensor_tensor(c0[:], oh0[:], wide(p0[:]), ALU.mult)
                link(v.tensor_tensor(c1[:], oh1[:], wide(p1[:]), ALU.mult))
                v.tensor_tensor(rows[:, :, COMB:COMB + EXPERTS], c0[:], c1[:], ALU.add)
                v.tensor_copy(rows[:, :, TOK].bitcast(i32), tokno[:, bass.ds(PER * (s - 1), PER)])
                dve.wait_ge(s_R, s)
                link(v.tensor_tensor(place[:], pR.rearrange("p (t e) -> p t e", e=EXPERTS), region0[:], ALU.add))
                v.tensor_tensor(c0[:], place[:], oh0[:], ALU.mult)
                link(v.tensor_tensor(c1[:], place[:], oh1[:], ALU.mult))
                v.tensor_reduce(slots[:, 0, :], c0[:], AX.X, ALU.add)
                link(v.tensor_reduce(slots[:, 1, :], c1[:], AX.X, ALU.add))
                if isinstance(s, int):
                    assert base[0] == ROUTE * s
                v.tensor_copy(slots_i[:], slots[:]).then_inc(s_slots, 1)

            def steps(s, one, two):
                for t in range(PER + 2 if two else PER):
                    i1, i2 = PER * s + t, PER * (s - 1) + t
                    if one and t < PER:
                        dve.wait_ge(s_rs1, s + 1)
                        v.tensor_scalar(xn[:, t % 2, :], tile_of(xall, i1), mv1[:, bass.ds(i1, 1), 0],
                                        rs1[:, bass.ds(i1, 1)], ALU.subtract, ALU.mult).then_inc(s_xn, 1)
                    if two and t >= 2:
                        dve.wait_ge(s_rs3, i2 - 1)
                        v.tensor_scalar(z[:, t % 2, :], x2[:, t - 2, :], mv3[:, t - 2, 0:1], rs3[:, t - 2:t - 1],
                                        ALU.subtract, ALU.mult).then_inc(s_z, 1)
                    if two and t < PER:
                        dve.wait_ge(s_O, i2 + 1)
                        dve.nop(nofuse=True)
                        v.bn_stats(st2[:, t, :], pO).then_inc(s_st2, 1)
                        dve.wait_ge(s_st2, i2 + 1)
                        dve.nop(nofuse=True)
                        v.bn_aggr(mv2[:, t, :], st2[:, t, :]).then_inc(s_mv2, 1)
                        dve.wait_ge(s_mv2, i2 + 1)
                        v.tensor_scalar(ve2[:, t:t + 1], mv2[:, t, 1:2], EPS, None, ALU.add).then_inc(s_ve2, 1)
                    if one and t < PER:
                        dve.wait_ge(s_exp, i1 + 1)
                        v.tensor_scalar(eq[:, t % 2, :], eq[:, t % 2, :], 1.0, -1.0, ALU.min, ALU.add).then_inc(s_em1, 1)
                        dve.wait_ge(s_em1, i1 + 1)
                        v.scalar_tensor_tensor(q[:, t % 2, :], pQ[t % 2], 0.0, eq[:, t % 2, :], ALU.max, ALU.add)\
                         .then_inc(s_q, 1)
                    if two and t < PER:
                        dve.wait_ge(s_rs2, i2 + 1)
                        v.tensor_scalar(on[:, t % 2, :], pO, mv2[:, t, 0:1], rs2[:, t:t + 1], ALU.subtract, ALU.mult)\
                         .then_inc(s_on, 1)
                    if two and t >= 2:
                        dve.wait_ge(s_hi, i2 - 1)
                        v.scalar_tensor_tensor(rows[:, t - 2, LO:LO + E // 2].bitcast(f16), z[:, t % 2, :], XW,
                                               rows[:, t - 2, HI:HI + E // 2].bitcast(f16), ALU.mult, ALU.subtract)\
                         .then_inc(s_lo, 1)
                    if one and t < PER:
                        dve.wait_ge(s_tanh, i1 + 1)
                        v.scalar_tensor_tensor(tile_of(vuall, i1), tile_of(vuall, i1), 1.0, pVU[t % 2], ALU.add, ALU.mult)\
                         .then_inc(s_vu, 1)
                    if two and t < PER:
                        dve.wait_ge(s_onb, i2 + 1)
                        v.tensor_tensor(y[:, t % 2, :], on[:, t % 2, :],
                                        vuall[:, bass.ds(i2, 1), E:2 * E].rearrange("p a n -> p (a n)"),
                                        ALU.mult).then_inc(s_y, 1)
                    if two and 1 <= t <= PER:
                        dve.wait_ge(s_W, i2)
                        if t == 1:
                            dve.wait_ge(s_x2free, s)
                        v.tensor_tensor(x2[:, t - 1, :], pW, tile_of(xall, i2 - 1), ALU.add).then_inc(s_x2, 1)
                        dve.wait_ge(s_x2, i2)
                        dve.nop(nofuse=True)
                        v.bn_stats(st3[:, t - 1, :], x2[:, t - 1, :]).then_inc(s_st3, 1)
                        dve.wait_ge(s_st3, i2)
                        dve.nop(nofuse=True)
                        v.bn_aggr(mv3[:, t - 1, :], st3[:, t - 1, :]).then_inc(s_mv3, 1)
                        dve.wait_ge(s_mv3, i2)
                        v.tensor_scalar(ve3[:, t - 1:t], mv3[:, t - 1, 1:2], EPS, None, ALU.add).then_inc(s_ve3, 1)
                    if two and t < NCH:
                        chunk_low(FIRST - 1 + s, t)
                    if one and not two:
                        for n in range(FIRST * NCH * t // PER, FIRST * NCH * (t + 1) // PER):
                            chunk_low(n // NCH, n % NCH)
                    if two and t >= 2:
                        dve.wait_ge(s_G, i2 - 1)
                        v.tensor_copy(lg[:, t - 2, :], pG).then_inc(s_lg, 1)
                    if one and t == PER - 1:
                        dve.wait_ge(s_KV, PER * (s + 1))
                        v.tensor_tensor(kv[:], pKV, headmask[:], ALU.mult).then_inc(s_kv, 1)
                if two:
                    route(s)
            steps(0, True, False)
            for grp in range(1, GROUPS):
                ln1_stats(grp)
            with dve.Fori(1, GROUPS) as s:
                steps(s, True, True)
            steps(GROUPS, False, True)

            tab = [ROUTE * GROUPS]

            def link(ins):
                tab[0] += 1
                ins.then_inc(s_route, 1)
                dve.wait_ge(s_route, tab[0])
            BE = [P, BLOCKS, EXPERTS]
            dve.wait_ge(s_C, 1)
            link(v.tensor_copy(count[:], pC))
            link(v.tensor_tensor(over, count[:].unsqueeze(2).to_broadcast([P, EXPERTS, TILES]), thresholds[:], ALU.is_gt))
            link(v.tensor_reduce(nblk[:], over, AX.X, ALU.add))
            link(v.tensor_tensor_scan(ends[:], oneE[:], nblk[:], 0.0, ALU.mult, ALU.add))
            link(v.tensor_tensor(past, ends[:].unsqueeze(1).to_broadcast(BE), blockno[:], ALU.is_le))
            link(v.tensor_reduce(bexp, past, AX.X, ALU.add))
            link(v.tensor_tensor(past2, past, nblk[:].unsqueeze(1).to_broadcast(BE), ALU.mult))
            link(v.tensor_reduce(bstart, past2, AX.X, ALU.add))
            link(v.scalar_tensor_tensor(boff, bstart, -float(P), block128[:], ALU.mult, ALU.add))
            link(v.scalar_tensor_tensor(boff, bexp, float(REGION), boff, ALU.mult, ALU.add))
            link(v.tensor_scalar(boff_i[:], boff, float(SPARE), None, ALU.min))
            link(v.tensor_scalar(bexp_i[:], bexp, float(EXPERTS - 1), None, ALU.min))
            link(v.tensor_tensor(padoff_i[:], count[:], region0[:, 0, :], ALU.add))
            dve.sem_inc(s_table, 1)

            def rows_turned(j, par):
                dve.wait_ge(s_XB, j + 1)
                v.tensor_copy(xb[par], pXB).then_inc(s_xb, 1)

            def step(j, slot, head, tail):
                par = slot % 2
                dve.wait_ge(s_sil, j + 1)
                dve.wait_ge(s_H1, j + 1)
                v.scalar_tensor_tensor(inter[par], pH1[par], IW / (XW * WW), sil[par], ALU.mult, ALU.mult)\
                 .then_inc(s_inter, 1)
                if not head:
                    weigh(j - 1, (slot - 1) % SL)
                if not tail:
                    rows_turned(j + 1, 1 - par)
                dve.wait_ge(s_ih, j + 1)
                dve.wait_ge(s_IT, j + 1)
                v.tensor_tensor(il[par].rearrange("p k t -> p (k t)"), pIT, ih[par].rearrange("p k t -> p (k t)"),
                                ALU.subtract).then_inc(s_il, 1)

            def weigh(j, slot):
                e = dve.value_load(bexp_i[0:1, bass.ds(j, 1)], min_val=0, max_val=EXPERTS - 1)
                dve.wait_ge(s_Y, j + 1)
                v.tensor_scalar(ys[slot], pY[slot % 2], blk[slot][:, bass.ds(COMB + e, 1)], 1.0 / (IW * WW),
                                ALU.mult, ALU.mult).then_inc(s_ys, 1)
            rows_turned(0, 0)
            step(0, 0, True, False)
            with dve.Fori(0, (BLOCKS - 3) // SL) as k:
                for r in range(SL):
                    step(SL * k + 1 + r, (1 + r) % SL, False, False)
            step(BLOCKS - 2, (BLOCKS - 2) % SL, False, False)
            step(BLOCKS - 1, (BLOCKS - 1) % SL, False, True)
            weigh(BLOCKS - 1, (BLOCKS - 1) % SL)

        @block.tensor
        def _(pe):
            m = nc.tensor
            pe.wait_ge(s_const, CONST_STEPS)
            pe.wait_ge(s_gbh, 5)

            def turn(dst, src, done):
                for k in range(KT):
                    mm = m.transpose(dst[:, k * P:(k + 1) * P], src[:, k * P:(k + 1) * P], ident[:])
                mm.then_inc(done, 1)

            def project(dst, lhs, w, c0_, n, done):
                m.matmul(dst, ones16[0:3, :], bias3[:, c0_:c0_ + n], start=True, stop=False)
                for k in range(KT):
                    mm = m.matmul(dst, lhs[:, k, :], w[:, k, :], start=False, stop=(k == KT - 1))
                mm.then_inc(done, 1)

            def steps(s, one, two):
                for t in range(PER + 2 if two else PER):
                    i1, i2 = PER * s + t, PER * (s - 1) + t
                    if one and t < PER:
                        pe.wait_ge(s_xn, i1 + 1)
                        turn(pXT[t % 2], xn[:, t % 2, :], s_XT)
                    if two and 1 <= t <= PER:
                        pe.wait_ge(s_y, i2)
                        if t >= 2:
                            pe.wait_ge(s_x2, i2 - 1)
                        turn(pYT, y[:, (t - 1) % 2, :], s_YT)
                    if two and t < PER:
                        pe.wait_ge(s_kv, s)
                        if one or t == 0:
                            pe.wait_ge(s_qT, i1)
                        if t >= 1:
                            pe.wait_ge(s_on, i2)
                        for k in range(KT):
                            mm = m.matmul(pO[:, k * P:(k + 1) * P], qT[:, t, k, :], kv[:, k * P:(k + 1) * P],
                                          start=True, stop=True)
                        mm.then_inc(s_O, 1)
                    if one and t < PER:
                        pe.wait_ge(s_xT, i1 + 1)
                        if not two and t == 0:
                            pe.wait_ge(s_wA, 80)
                            pe.wait_ge(s_bias3, 48)
                        project(pQ[t % 2], xT[:, t % 2], wcat[:, :, 0:E], 0, E, s_Q)
                        project(pVU[t % 2], xT[:, t % 2], wcat[:, :, E:3 * E], E, 2 * E, s_VU)
                    if two and t >= 2:
                        pe.wait_ge(s_z, i2 - 1)
                        if t >= 3:
                            pe.wait_ge(s_lg, i2 - 2)
                        turn(pZT, z[:, t % 2, :], s_ZT)
                    if two and 1 <= t <= PER:
                        pe.wait_ge(s_yT, i2)
                        project(pW, yT, wout, 3 * E, E, s_W)
                    if one and t < PER:
                        pe.wait_ge(s_q, i1 + 1)
                        pe.wait_ge(s_vu, i1 + 1)
                        if t == 0 and two:
                            pe.wait_ge(s_kv, s)
                        for k in range(KT):
                            mm = m.matmul(pKV[:, k * P:(k + 1) * P], q[:, t % 2, k * P:(k + 1) * P],
                                          vuall[:, bass.ds(i1, 1), k * P:(k + 1) * P].rearrange("p a n -> p (a n)"),
                                          start=(t == 0 and k == 0), stop=(t == PER - 1), skip_group_check=True)
                        mm.then_inc(s_KV, 1)
                        if two:
                            pe.wait_ge(s_on, i2 + 1)
                        turn(pQT, q[:, t % 2, :], s_QT)
                    if two and t >= 2:
                        pe.wait_ge(s_zT, i2 - 1)
                        for k in range(KT):
                            mm = m.matmul(pG, zT[:, k, :], gatew[:, k, :], start=(k == 0), stop=(k == KT - 1))
                        mm.then_inc(s_G, 1)
                if two:
                    pe.wait_ge(s_chosen, s)
                    m.matmul(pR, before[:], chosen[:].rearrange("p t e -> p (t e)"), start=True, stop=False)
                    m.matmul(pR, ones16[:], sofar[:, 0:PER, :].rearrange("p t e -> p (t e)"), start=False, stop=True)\
                     .then_inc(s_R, 1)
            steps(0, True, False)
            with pe.Fori(1, GROUPS) as s:
                steps(s, True, True)
            steps(GROUPS, False, True)
            m.matmul(pC, ones16[:], sofar[:, PER, :], start=True, stop=True).then_inc(s_C, 1)

            def turn_rows(j, slot, uses):
                pe.wait_ge(s_blk[slot], 16 * uses)
                r16 = blk[slot][:, 0:E].bitcast(f16)
                for k in range(2 * KT):
                    mm = m.transpose(pXB[:, k, :], r16[:, k * P:(k + 1) * P], ident16[:])
                mm.then_inc(s_XB, 1)

            def three(dst, pairs, done):
                last = len(pairs) * 3 - 1
                n = 0
                for hi, lo_, wh, wl in pairs:
                    for l, r in ((hi, wh), (hi, wl), (lo_, wh)):
                        mm = m.matmul(dst, l, r, start=(n == 0), stop=(n == last))
                        n += 1
                mm.then_inc(done, 1)

            def up(j, slot, e):
                par = slot % 2
                pe.wait_ge(s_xb, j + 1)
                for c, dst, done in ((0, pH0[par], s_H0), (1, pH1[par], s_H1)):
                    three(dst, [(xb[par][:, k, :], xb[par][:, KT + k, :],
                                 weights_of(w_hi, e, c * CH + k * MLP, MLP), weights_of(w_lo, e, c * CH + k * MLP, MLP))
                                for k in range(KT)], done)

            def turn_inter(j, slot):
                par = slot % 2
                pe.wait_ge(s_inter, j + 1)
                for k in range(MT):
                    mm = m.transpose(pIT[:, k * P:(k + 1) * P], inter[par][:, k * P:(k + 1) * P], ident[:])
                mm.then_inc(s_IT, 1)

            def down(j, slot):
                par = slot % 2
                e = pe.value_load(bexp_i[0:1, bass.ds(j, 1)], min_val=0, max_val=EXPERTS - 1)
                pe.wait_ge(s_il, j + 1)
                three(pY[par], [(ih[par][:, k, :], il[par][:, k, :], weights_of(w_hi, e, 2 * CH + k * E, E),
                                 weights_of(w_lo, e, 2 * CH + k * E, E)) for k in range(MT)], s_Y)

            def step(j, slot, uses, head, tail):
                e = pe.value_load(bexp_i[0:1, bass.ds(j, 1)], min_val=0, max_val=EXPERTS - 1)
                up(j, slot, e)
                if not head:
                    down(j - 1, (slot - 1) % SL)
                if not tail:
                    turn_rows(j + 1, (slot + 1) % SL, uses)
                turn_inter(j, slot)
            pe.wait_ge(s_table, 1)
            pe.wait_ge(s_wlo, NCH * EXPERTS)
            turn_rows(0, 0, 1)
            step(0, 0, 1, True, False)
            with pe.Fori(0, (BLOCKS - 3) // SL) as k:
                for r in range(SL):
                    step(SL * k + 1 + r, (1 + r) % SL, k + (r + 2) // SL + 1, False, False)
            step(BLOCKS - 2, (BLOCKS - 2) % SL, (BLOCKS - 1) // SL + 1, False, False)
            step(BLOCKS - 1, (BLOCKS - 1) % SL, 0, False, True)
            down(BLOCKS - 1, (BLOCKS - 1) % SL)


_INS = ['x', 'Wqk', 'bqk', 'Wv', 'bv', 'Wu', 'bu', 'Wo', 'bo', 'ln_g', 'ln_b']
_FFN = ['gate_kernel', 'w0_kernel', 'w1_kernel', 'wo_kernel']


def kernel(**inputs):
    import numpy as _np
    import concourse.bacc as _bacc
    from concourse import mybir as _mybir
    from concourse.bass_utils import run_bass_kernel_spmd as _run

    nc = _bacc.Bacc("TRN2", target_bir_lowering=False, num_devices=1)
    arrays, args = {}, []
    for name in ['L0_attn_' + n for n in _INS] + ['L0_ffn_' + n for n in _FFN]:
        a = _np.ascontiguousarray(inputs[name])
        if name == 'L0_attn_x':
            batch, seq, width = a.shape
            a = a.reshape(batch * seq, width)
        arrays["in_" + name] = a
        args.append(nc.dram_tensor("in_" + name, a.shape, _mybir.dt.from_np(a.dtype), kind="ExternalInput").ap())
    out = nc.dram_tensor("out_0", (batch * seq + 128, width), _mybir.dt.float32, kind="ExternalOutput").ap()
    linear_attention_then_top2_moe(nc, *args, out)
    r = _run(nc, [arrays], core_ids=[0])
    return r.results[0]["out_0"][:batch * seq].reshape(batch, seq, width)
```

```python
import concourse.bass as bass
from concourse import mybir
from contextlib import ExitStack


def linear_attention_then_top2_moe(nc, x, Wqk, bqk, Wv, bv, Wu, bu, Wo, bo, ln_g, ln_b, gate, w0, w1, wo, out):
    f32, f16, bf16, i32 = mybir.dt.float32, mybir.dt.float16, mybir.dt.bfloat16, mybir.dt.int32
    ALU, ACT, AX = mybir.AluOpType, mybir.ActivationFunctionType, mybir.AxisListType

    P = 128
    T, E = x.shape
    EXPERTS, _, MLP = w0.shape
    TILES = T // P
    PER = 4
    GROUPS = TILES // PER
    DH = 16
    KT = E // P
    MT = MLP // P
    EPS = 1e-5
    TOP = 2
    REGION = T + P
    SPARE = EXPERTS * REGION
    BLOCKS = (TOP * T + EXPERTS * (P - 1)) // P
    XW, WW, IW = 256.0, 256.0, 64.0

    HI, LO, COMB, TOK, ROW = 0, E // 2, E, E + EXPERTS, E + 16
    CH = 1024
    NCH = 3
    EW = NCH * CH

    sent = nc.dram_tensor("sent", (SPARE + P, ROW), f32).ap()

    ctx = ExitStack()
    with ctx:
        def sb(name, shape, dt):
            return ctx.enter_context(nc.sbuf_tensor(name, shape, dt))

        def pb(name, shape, dt):
            return ctx.enter_context(nc.psum_tensor(name, shape, dt))

        def sem(name):
            return ctx.enter_context(nc.semaphore(name))

        ident = sb("ident", [P, P], f32)
        ident16 = sb("ident16", [P, P], f16)
        before = sb("before", [P, P], bf16)
        ones16 = sb("ones16", [P, P], bf16)
        headmask = sb("headmask", [P, KT * P], f32)
        neghalf = sb("neghalf", [P, TILES], f32)
        desc = sb("desc", [P, PER, EXPERTS], f32)
        region0 = sb("region0", [P, PER, EXPERTS], f32)
        thresholds = sb("thresholds", [P, EXPERTS, TILES], f32)
        blockno = sb("blockno", [P, BLOCKS, EXPERTS], f32)
        block128 = sb("block128", [P, BLOCKS], f32)
        oneE = sb("oneE", [P, EXPERTS], f32)
        tokno = sb("tokno", [P, TILES], i32)
        padrows = sb("padrows", [P, ROW], f32)
        gamma = sb("gamma", [P, E], f32)
        beta = sb("beta", [P, E], f32)
        wcat = sb("wcat", [P, KT, 3 * E], f32)
        wout = sb("wout", [P, KT, E], f32)
        gatew = sb("gatew", [P, KT, EXPERTS], f32)
        bias3 = sb("bias3", [3, 4 * E], bf16)
        stage = sb("stage", [P, NCH, CH], f32)
        w_hi = sb("w_hi", [P, EXPERTS, EW], f16)
        w_lo = sb("w_lo", [P, EXPERTS, EW], f16)
        room = sb("room", [P, 2 * TILES * E], f32)
        xall = room[:, 0:TILES * E].rearrange("p (t e) -> p t e", e=E)
        uring = room[:, TILES * E:TILES * E + 8 * E].rearrange("p (t e) -> p t e", e=E)
        spare_room = (TILES + 8) * E
        brow = room[0:1, spare_room:spare_room + 4 * E]
        brest = uring[0:1, 4:8, :].rearrange("p t e -> p (t e)")
        bpart = room[0:1, spare_room + 4 * E:spare_room + 8 * E].bitcast(bf16)
        bpart2 = uring[0:1, 2:4, :].rearrange("p t e -> p (t e)").bitcast(bf16)
        bparts = [bpart[:, 0:4 * E], bpart[:, 4 * E:8 * E], bpart2]
        st1 = sb("st1", [P, TILES, 6], f32)
        mv1 = sb("mv1", [P, TILES, 2], f32)
        ve1 = sb("ve1", [P, TILES], f32)
        rs1 = sb("rs1", [P, TILES], f32)
        nm1 = sb("nm1", [P, TILES], f32)
        xn = sb("xn", [P, 2, E], f32)
        xT = sb("xT", [P, 2, KT, P], f32)
        eq = sb("eq", [P, 2, E], f32)
        th = sb("th", [P, 2, 2 * E], f32)
        q = sb("q", [P, 2, E], f32)
        vv = sb("vv", [P, 2, E], f32)
        QR = 8
        qT = sb("qT", [P, QR, KT * P], f32)
        kv = sb("kv", [P, 2, KT * P], f32)
        st2 = sb("st2", [P, 2, 6], f32)
        mv2 = sb("mv2", [P, 2, 2], f32)
        ve2 = sb("ve2", [P, 2], f32)
        rs2 = sb("rs2", [P, 2], f32)
        nm2 = sb("nm2", [P, 2], f32)
        on = sb("on", [P, 2, E], f32)
        yT = sb("yT", [P, KT * P], f32)
        x2 = sb("x2", [P, PER, E], f32)
        st3 = sb("st3", [P, 2, 6], f32)
        mv3 = sb("mv3", [P, 2, 2], f32)
        ve3 = sb("ve3", [P, 2], f32)
        rs3 = sb("rs3", [P, 2], f32)
        z = sb("z", [P, 2, E], f32)
        zT = sb("zT", [P, KT * P], f32)
        rows = sb("rows", [P, QR, ROW], f32)
        lg = sb("lg", [P, PER, EXPERTS], f32)
        lg2 = sb("lg2", [P, PER, EXPERTS], f32)
        same = sb("same", [P, PER, EXPERTS], f32)
        first = sb("first", [P, PER, EXPERTS], f32)
        oh0 = sb("oh0", [P, PER, EXPERTS], f32)
        oh1 = sb("oh1", [P, PER, EXPERTS], f32)
        c0 = sb("c0", [P, PER, EXPERTS], f32)
        c1 = sb("c1", [P, PER, EXPERTS], f32)
        chosen = sb("chosen", [P, PER, EXPERTS], bf16)
        sofar = sb("sofar", [P, 2, PER + 1, EXPERTS], bf16)
        m0 = sb("m0", [P, PER], f32)
        m1 = sb("m1", [P, PER], f32)
        k0 = sb("k0", [P, PER], f32)
        dm = sb("dm", [P, PER], f32)
        ex = sb("ex", [P, PER], f32)
        p0 = sb("p0", [P, PER], f32)
        p1 = sb("p1", [P, PER], f32)
        place = sb("place", [P, PER, EXPERTS], f32)
        slots = sb("slots", [P, TOP, PER], f32)
        slots_i = sb("slots_i", [P, 2, TOP, PER], i32)
        count = sb("count", [P, EXPERTS], f32)
        nblk = sb("nblk", [P, EXPERTS], f32)
        ends = sb("ends", [P, EXPERTS], f32)
        padoff = sb("padoff", [P, EXPERTS], f32)
        bexp_i = sb("bexp_i", [P, BLOCKS], i32)
        boff_i = sb("boff_i", [P, BLOCKS], i32)
        padoff_i = sb("padoff_i", [P, EXPERTS], i32)
        at = [0]

        def cut(words):
            at[0] += words
            return room[:, at[0] - words:at[0]]
        SL = 4
        blk = [cut(ROW) for _ in range(SL)]
        sil = [cut(MLP) for _ in range(2)]
        inter = [cut(MLP) for _ in range(2)]
        xb = [cut(2 * KT * P // 2).bitcast(f16).rearrange("p (k t) -> p k t", t=P) for _ in range(2)]
        ih = [cut(MLP // 2).bitcast(f16).rearrange("p (k t) -> p k t", t=P) for _ in range(2)]
        il = [cut(MLP // 2).bitcast(f16).rearrange("p (k t) -> p k t", t=P) for _ in range(2)]
        ys = [cut(E) for _ in range(SL)]
        over = cut(EXPERTS * TILES).rearrange("p (e t) -> p e t", t=TILES)
        past = cut(BLOCKS * EXPERTS).rearrange("p (j e) -> p j e", e=EXPERTS)
        past2 = cut(BLOCKS * EXPERTS).rearrange("p (j e) -> p j e", e=EXPERTS)
        bexp = cut(BLOCKS)
        bstart = cut(BLOCKS)
        boff = cut(BLOCKS)
        assert at[0] <= 2 * TILES * E

        bank = [pb(f"bank{n}", [P, 512], f32) for n in range(8)]
        pVU = [bank[0][:, :], bank[1][:, :]]
        pQ = [bank[2][:, 0:E], bank[3][:, 0:E]]
        pXT = [bank[2][:, E:2 * E], bank[3][:, E:2 * E]]
        pKV = bank[4][:, 0:KT * P]
        pQT = pXT
        pO = bank[5][:, 0:E]
        pYT = bank[6][:, 0:E]
        pW = bank[6][:, E:2 * E]
        pZT = bank[7][:, 0:E]
        pG = bank[7][:, E:E + EXPERTS]
        pR = bank[7][:, 320:320 + PER * EXPERTS]
        pC = bank[4][:, 384:384 + EXPERTS]
        pH0 = [bank[0][:, :], bank[2][:, :]]
        pH1 = [bank[1][:, :], bank[3][:, :]]
        pXB = bank[4][:, 0:KT * P].bitcast(f16).rearrange("p (k t) -> p k t", t=P)
        pIT = bank[5][:, :]
        pY = [bank[6][:, 0:E], bank[7][:, 0:E]]

        s_const = sem("s_const")
        s_xin = [sem(f"s_xin{g}") for g in range(GROUPS)]
        s_wA = sem("s_wA")
        s_brow = sem("s_brow")
        s_bsplit = sem("s_bsplit")
        s_bias3 = sem("s_bias3")
        s_gb = sem("s_gb")
        s_gbh = sem("s_gbh")
        s_stage = [sem(f"s_stage{n}") for n in range(NCH)]
        s_whi = sem("s_whi")
        s_wlo = sem("s_wlo")
        s_st1 = sem("s_st1")
        s_mv1 = sem("s_mv1")
        s_ve1 = sem("s_ve1")
        s_rs1 = sem("s_rs1")
        s_xn = sem("s_xn")
        s_XT = sem("s_XT")
        s_xT = sem("s_xT")
        s_Q = sem("s_Q")
        s_VU = sem("s_VU")
        s_exp = sem("s_exp")
        s_tanh = sem("s_tanh")
        s_em1 = sem("s_em1")
        s_q = sem("s_q")
        s_v = sem("s_v")
        s_u = sem("s_u")
        s_KV = sem("s_KV")
        s_QT = sem("s_QT")
        s_qT = sem("s_qT")
        s_kv = sem("s_kv")
        s_O = sem("s_O")
        s_st2 = sem("s_st2")
        s_mv2 = sem("s_mv2")
        s_ve2 = sem("s_ve2")
        s_rs2 = sem("s_rs2")
        s_nm2 = sem("s_nm2")
        s_on = sem("s_on")
        s_ong = sem("s_ong")
        s_onb = sem("s_onb")
        s_y = sem("s_y")
        s_YT = sem("s_YT")
        s_yT = sem("s_yT")
        s_W = sem("s_W")
        s_x2 = sem("s_x2")
        s_st3 = sem("s_st3")
        s_mv3 = sem("s_mv3")
        s_ve3 = sem("s_ve3")
        s_rs3 = sem("s_rs3")
        s_z = sem("s_z")
        s_hi = sem("s_hi")
        s_lo = sem("s_lo")
        s_ZT = sem("s_ZT")
        s_zT = sem("s_zT")
        s_G = sem("s_G")
        s_lg = sem("s_lg")
        s_route = sem("s_route")
        s_oh = sem("s_oh")
        s_meta = sem("s_meta")
        s_dm = sem("s_dm")
        s_ex = sem("s_ex")
        s_chosen = sem("s_chosen")
        s_R = sem("s_R")
        s_slots = sem("s_slots")
        s_sent = [sem(f"s_sent{n}") for n in range(QR)]
        s_store = [sem(f"s_store{n}") for n in range(PER)]
        s_spare = sem("s_spare")
        s_C = sem("s_C")
        s_table = sem("s_table")
        s_padA = sem("s_padA")
        s_padS = sem("s_padS")
        s_blk = [sem(f"s_blk{n}") for n in range(SL)]
        s_XB = sem("s_XB")
        s_xb = sem("s_xb")
        s_H0 = sem("s_H0")
        s_H1 = sem("s_H1")
        s_sil = sem("s_sil")
        s_inter = sem("s_inter")
        s_IT = sem("s_IT")
        s_ih = sem("s_ih")
        s_il = sem("s_il")
        s_Y = sem("s_Y")
        s_ys = sem("s_ys")
        s_added = sem("s_added")

        block = ctx.enter_context(nc.Block())

        CONST_STEPS = 19

        def weights_of(part, e, c0_, n):
            return part[:, bass.ds(e, 1), c0_:c0_ + n].rearrange("p a n -> p (a n)")

        def chunk_source(e, c):
            return (w0, w1, wo)[c][e, :, :].rearrange("(k p) n -> p k n", p=P)

        def chunk_view(c):
            w = MLP if c < 2 else E
            return stage[:, c, :].rearrange("p (k n) -> p k n", n=w)

        GROUP = [(0, 4), (4, 4), (8, 4), (12, 2), (14, 2)]
        FIRST_STEP, STEPS = -1, TILES + 12
        NCHUNK = NCH * EXPERTS

        def live(i):
            return 0 <= i < TILES

        def chunks_of(i):
            return range(2 * i, 2 * i + 2) if 0 <= i < 4 else [i + 4] if 4 <= i < NCHUNK - 4 else []

        def routed(i, lag):
            for n, (t0, nt) in enumerate(GROUP):
                if t0 + nt - 1 == i - lag:
                    return n
            return None

        def group_of(tile):
            return max(n for n, (t0, _) in enumerate(GROUP) if t0 <= tile)

        @block.sync
        def _(sp):
            for g in range(GROUPS):
                sp.dma_start(xall[:, PER * g:PER * g + PER, :],
                             x[P * PER * g:P * PER * (g + 1), :].rearrange("(t p) e -> p t e", p=P)).then_inc(s_xin[g], 16)
                if g == 0:
                    sp.dma_start(brow[:, 0:E], bqk.rearrange("(a n) -> a n", a=1)).then_inc(s_brow, 16)
                    sp.dma_start(brow[:, E:2 * E], bv.rearrange("(a n) -> a n", a=1)).then_inc(s_brow, 16)
                    sp.dma_start(brow[:, 2 * E:3 * E], bu.rearrange("(a n) -> a n", a=1)).then_inc(s_brow, 16)
                    sp.dma_start(brow[:, 3 * E:4 * E], bo.rearrange("(a n) -> a n", a=1)).then_inc(s_brow, 16)
            for n in range(NCH):
                sp.dma_start(chunk_view(n), chunk_source(0, n)).then_inc(s_stage[n], 16)
            sp.wait_ge(s_bsplit, 5)
            for n in range(3):
                sp.dma_start(bias3[n:n + 1, :], bparts[n]).then_inc(s_bias3, 16)
            for i in range(0, STEPS):
                for n in chunks_of(i):
                    if n + NCH < NCHUNK:
                        sp.wait_ge(s_wlo, n + 1)
                        sp.dma_start(chunk_view(n % NCH), chunk_source((n + NCH) // NCH, n % NCH))\
                          .then_inc(s_stage[n % NCH], 16)
                if i == 2:
                    sp.wait_ge(s_const, CONST_STEPS)
                    sp.dma_start(sent[SPARE:SPARE + P, :], padrows[:, :]).then_inc(s_spare, 16)
                    sp.dma_start(out[T:T + P, :], padrows[:, 0:E]).then_inc(s_spare, 16)
                if live(i - 8):
                    sp.wait_ge(s_x2, i - 7)
                    sp.dma_start(out[(i - 8) * P:(i - 7) * P, :], x2[:, (i - 8) % PER, :]).then_inc(s_store[(i - 8) % PER], 16)
            sp.wait_ge(s_table, 1)
            for e in range(EXPERTS // 2, EXPERTS):
                off = sp.value_load(padoff_i[0:1, e:e + 1], min_val=0, max_val=SPARE - P)
                sp.dma_start(sent[bass.ds(off, P), :], padrows[:, :]).then_inc(s_padS, 16)
            sp.wait_ge(s_padS, 16 * (EXPERTS // 2))
            sp.wait_ge(s_padA, 16 * (EXPERTS // 2))
            sp.wait_ge(s_spare, 32)
            for n in range(QR):
                sp.wait_ge(s_sent[n], 16 * TOP * TILES // QR)

            def load(j, slot):
                off = sp.value_load(boff_i[0:1, bass.ds(j, 1)], min_val=0, max_val=SPARE)
                sp.dma_start(blk[slot], sent[bass.ds(off, P), :]).then_inc(s_blk[slot], 16)
            for j in range(SL):
                load(j, j)
            with sp.Fori(0, (BLOCKS - SL) // SL) as k:
                for r in range(SL):
                    sp.wait_ge(s_added, 16 * (SL * k + r + 1))
                    load(SL * k + SL + r, r)
            for j in range(BLOCKS - (BLOCKS - SL) % SL, BLOCKS):
                sp.wait_ge(s_added, 16 * (j - SL + 1))
                load(j, j % SL)
            sp.wait_ge(s_added, 16 * BLOCKS)

        @block.gpsimd
        def _(pool):
            g = nc.gpsimd
            g.memset(ident[:], 0.0).then_inc(s_const, 1)
            g.memset(ident16[:], 0.0).then_inc(s_const, 1)
            g.memset(before[:], 1.0).then_inc(s_const, 1)
            g.memset(headmask[:], 0.5).then_inc(s_const, 1)
            g.memset(neghalf[:], -0.5).then_inc(s_const, 1)
            pool.wait_ge(s_const, 5)
            g.affine_select(out=ident[:], in_=ident[:], compare_op=ALU.not_equal, fill=1.0, base=0,
                            pattern=[[-1, P]], channel_multiplier=1).then_inc(s_const, 1)
            g.affine_select(out=ident16[:], in_=ident16[:], compare_op=ALU.not_equal, fill=1.0, base=0,
                            pattern=[[-1, P]], channel_multiplier=1).then_inc(s_const, 1)
            g.affine_select(out=before[:], in_=before[:], compare_op=ALU.is_gt, fill=0.0, base=0,
                            pattern=[[1, P]], channel_multiplier=-1).then_inc(s_const, 1)
            hm = headmask[:].rearrange("p (k a c) -> p k a c", k=KT, c=DH)
            g.affine_select(out=hm, in_=hm, compare_op=ALU.is_ge, fill=0.0, base=0,
                            pattern=[[0, KT], [-DH, P // DH], [0, DH]], channel_multiplier=1).then_inc(s_const, 1)

            def ln1_scale(n):
                at_ = slice(PER * n, PER * n + PER)
                pool.wait_ge(s_ve1, n + 1)
                g.tensor_tensor(rs1[:, at_], ve1[:, at_], neghalf[:, 0:PER], ALU.pow).then_inc(s_rs1, 1)
                pool.wait_ge(s_rs1, 3 * n + 1)
                g.tensor_tensor(nm1[:, at_], mv1[:, at_, 0], rs1[:, at_], ALU.mult).then_inc(s_rs1, 1)
                pool.wait_ge(s_rs1, 3 * n + 2)
                g.tensor_scalar(nm1[:, at_], nm1[:, at_], -1.0, 1.0, ALU.mult, ALU.mult).then_inc(s_rs1, 1)
            ln1_scale(0)
            pool.wait_ge(s_const, 9)
            g.affine_select(out=hm, in_=hm, compare_op=ALU.is_ge, fill=0.0, base=DH - 1,
                            pattern=[[0, KT], [DH, P // DH], [0, DH]], channel_multiplier=-1).then_inc(s_const, 1)
            g.iota(desc[:], [[0, PER], [-1, EXPERTS]], base=EXPERTS, channel_multiplier=0,
                   allow_small_or_imprecise_dtypes=True).then_inc(s_const, 1)
            g.iota(region0[:], [[0, PER], [REGION, EXPERTS]], base=0, channel_multiplier=0,
                   allow_small_or_imprecise_dtypes=True).then_inc(s_const, 1)
            g.iota(thresholds[:], [[0, EXPERTS], [P, TILES]], base=0, channel_multiplier=0,
                   allow_small_or_imprecise_dtypes=True).then_inc(s_const, 1)
            g.iota(blockno[:], [[1, BLOCKS], [0, EXPERTS]], base=0, channel_multiplier=0,
                   allow_small_or_imprecise_dtypes=True).then_inc(s_const, 1)
            g.iota(block128[:], [[P, BLOCKS]], base=0, channel_multiplier=0,
                   allow_small_or_imprecise_dtypes=True).then_inc(s_const, 1)
            g.iota(tokno[:], [[P, TILES]], base=0, channel_multiplier=1).then_inc(s_const, 1)
            g.memset(padrows[:], 0.0).then_inc(s_const, 1)
            pool.wait_ge(s_const, 17)
            g.iota(padrows[:, TOK:TOK + 1].bitcast(i32), [[0, 1]], base=T, channel_multiplier=1).then_inc(s_const, 1)
            g.memset(rows[:], 0.0).then_inc(s_const, 1)
            pool.wait_ge(s_gbh, 2)
            for i in range(0, STEPS):
                if i % PER == 1 and i // PER + 1 < GROUPS:
                    ln1_scale(i // PER + 1)
                if live(i - 8):
                    n = (i - 8) % 2
                    pool.wait_ge(s_mv3, i - 7)
                    g.tensor_scalar(ve3[:, n:n + 1], mv3[:, n, 1:2], 1.0, EPS, ALU.mult, ALU.add).then_inc(s_ve3, 1)
                    pool.wait_ge(s_ve3, i - 7)
                    g.tensor_tensor(rs3[:, n:n + 1], ve3[:, n:n + 1], neghalf[:, 0:1], ALU.pow).then_inc(s_rs3, 1)
                if live(i - 6):
                    n = i % 2
                    pool.wait_ge(s_on, i - 5)
                    g.tensor_tensor(on[:, n, :], on[:, n, :], gamma[:], ALU.mult).then_inc(s_ong, 1)
                    pool.wait_ge(s_ong, i - 5)
                    g.tensor_tensor(on[:, n, :], on[:, n, :], beta[:], ALU.add).then_inc(s_onb, 1)
                if live(i - 5):
                    n = (i - 5) % 2
                    pool.wait_ge(s_mv2, i - 4)
                    g.tensor_scalar(ve2[:, n:n + 1], mv2[:, n, 1:2], 1.0, EPS, ALU.mult, ALU.add).then_inc(s_ve2, 1)
                    pool.wait_ge(s_ve2, i - 4)
                    g.tensor_tensor(rs2[:, n:n + 1], ve2[:, n:n + 1], neghalf[:, 0:1], ALU.pow).then_inc(s_rs2, 1)
                    pool.wait_ge(s_rs2, i - 4)
                    g.tensor_scalar(nm2[:, n:n + 1], mv2[:, n, 0:1], rs2[:, n:n + 1], -1.0, ALU.mult, ALU.mult)\
                     .then_inc(s_nm2, 1)
                for n, (t0, nt) in enumerate(GROUP):
                    k = i - (t0 + nt + 10)
                    if 0 <= k < nt:
                        pool.wait_ge(s_slots, n + 1)
                        for c in range(TOP):
                            g.indirect_dma_start(sent, bass.IndirectOffsetOnAxis(slots_i[:, n % 2, c, k:k + 1], 0),
                                                 rows[:, (t0 + k) % QR, :], None).then_inc(s_sent[(t0 + k) % QR], 16)

            for n in range(PER):
                pool.wait_ge(s_store[n], 16 * TILES // PER)
            pool.wait_ge(s_spare, 32)

            def add_block(j, slot, head):
                pool.wait_ge(s_ys, j + 1)
                if not head:
                    pool.wait_ge(s_added, 16 * j)
                pool.nop(nofuse=True)
                g.indirect_dma_start(out, bass.IndirectOffsetOnAxis(blk[slot][:, TOK:TOK + 1].bitcast(i32), 0),
                                     ys[slot], None, compute_op=ALU.add).then_inc(s_added, 16)
            add_block(0, 0, True)
            with pool.Fori(0, (BLOCKS - 3) // SL) as k:
                for r in range(SL):
                    add_block(SL * k + 1 + r, (1 + r) % SL, False)
            for j in range(BLOCKS - 2, BLOCKS):
                add_block(j, j % SL, False)

        @block.scalar
        def _(act):
            a = nc.scalar
            for src, lo_ in ((Wqk, 0), (Wv, E), (Wu, 2 * E)):
                act.dma_start(wcat[:, :, lo_:lo_ + E], src.rearrange("(k p) n -> p k n", p=P)).then_inc(s_wA, 16)
            act.dma_start(wout[:], Wo.rearrange("(k p) n -> p k n", p=P)).then_inc(s_wA, 16)
            act.dma_start(gatew[:], gate.rearrange("(k p) n -> p k n", p=P)).then_inc(s_wA, 16)
            act.dma_start(gamma[:], ln_g.rearrange("(a n) -> a n", a=1).broadcast_to([P, E])).then_inc(s_gb, 16)
            act.dma_start(beta[:], ln_b.rearrange("(a n) -> a n", a=1).broadcast_to([P, E])).then_inc(s_gb, 16)

            def chunk_high(n):
                act.wait_ge(s_stage[n % NCH], 16 * (n // NCH + 1))
                a.activation(w_hi[:, n // NCH, n % NCH * CH:n % NCH * CH + CH], stage[:, n % NCH, :], ACT.Copy,
                             scale=WW).then_inc(s_whi, 1)

            for i in range(FIRST_STEP, STEPS):
                if live(i + 1):
                    act.wait_ge(s_rs1, 3 * ((i + 1) // PER + 1))
                    a.activation(xn[:, (i + 1) % 2, :], xall[:, i + 1, :], ACT.Identity, scale=rs1[:, i + 1:i + 2],
                                 bias=nm1[:, i + 1:i + 2]).then_inc(s_xn, 1)
                if live(i - 6):
                    n = i % 2
                    act.wait_ge(s_nm2, i - 5)
                    a.activation(on[:, n, :], pO, ACT.Identity, scale=rs2[:, n:n + 1], bias=nm2[:, n:n + 1]).then_inc(s_on, 1)
                if live(i - 9):
                    if i - 9 >= QR:
                        act.wait_ge(s_sent[(i - 9) % QR], 16 * TOP)
                    act.wait_ge(s_z, i - 8)
                    a.activation(rows[:, (i - 9) % QR, HI:HI + E // 2].bitcast(f16), z[:, (i - 9) % 2, :], ACT.Copy,
                                 scale=XW).then_inc(s_hi, 1)
                if live(i):
                    act.wait_ge(s_Q, i + 1)
                    a.activation(eq[:, i % 2, :], pQ[i % 2], ACT.Exp).then_inc(s_exp, 1)
                for n in chunks_of(i):
                    chunk_high(n)
                if live(i):
                    act.wait_ge(s_VU, i + 1)
                    a.activation(th[:, i % 2, :], pVU[i % 2], ACT.Tanh, scale=0.5).then_inc(s_tanh, 1)
                if live(i - 7):
                    act.wait_ge(s_YT, i - 6)
                    a.activation(yT[:], pYT, ACT.Copy).then_inc(s_yT, 1)
                if live(i - 1):
                    act.wait_ge(s_QT, i)
                    a.activation(qT[:, (i - 1) % QR, :], pQT[(i - 1) % 2], ACT.Copy).then_inc(s_qT, 1)
                if live(i - 9):
                    act.wait_ge(s_ZT, i - 8)
                    a.activation(zT[:], pZT, ACT.Copy).then_inc(s_zT, 1)
                if live(i + 1):
                    act.wait_ge(s_XT, i + 2)
                    a.activation(xT[:, (i + 1) % 2, :, :].rearrange("p k t -> p (k t)"), pXT[(i + 1) % 2], ACT.Copy)\
                     .then_inc(s_xT, 1)
                n = routed(i, 10)
                if n is not None:
                    act.wait_ge(s_dm, n + 1)
                    a.activation(ex[:, 0:GROUP[n][1]], dm[:, 0:GROUP[n][1]], ACT.Exp).then_inc(s_ex, 1)

            act.wait_ge(s_table, 1)
            for e in range(EXPERTS // 2):
                off = act.value_load(padoff_i[0:1, e:e + 1], min_val=0, max_val=SPARE - P)
                act.dma_start(sent[bass.ds(off, P), :], padrows[:, :]).then_inc(s_padA, 16)

            def step(j, par):
                act.wait_ge(s_H0, j + 1)
                a.activation(sil[par], pH0[par], ACT.Silu, scale=1.0 / (XW * WW)).then_inc(s_sil, 1)
                act.wait_ge(s_IT, j + 1)
                a.activation(ih[par].rearrange("p k t -> p (k t)"), pIT, ACT.Copy).then_inc(s_ih, 1)
            step(0, 0)
            with act.Fori(0, (BLOCKS - 3) // SL) as k:
                for r in range(SL):
                    step(SL * k + 1 + r, (1 + r) % 2)
            for j in range(BLOCKS - 2, BLOCKS):
                step(j, j % 2)

        @block.vector
        def _(dve):
            v = nc.vector

            def ln1_stats(grp):
                dve.wait_ge(s_xin[grp], 16)
                for i in range(PER * grp, PER * grp + PER):
                    v.bn_stats(st1[:, i, :], xall[:, i, :]).then_inc(s_st1, 1)
                for i in range(PER * grp, PER * grp + PER):
                    dve.wait_ge(s_st1, i + 1)
                    v.bn_aggr(mv1[:, i, :], st1[:, i, :]).then_inc(s_mv1, 1)
                dve.wait_ge(s_mv1, PER * grp + PER)
                v.tensor_scalar(ve1[:, PER * grp:PER * grp + PER], mv1[:, PER * grp:PER * grp + PER, 1], EPS, None,
                                ALU.add).then_inc(s_ve1, 1)
            ln1_stats(0)
            dve.wait_ge(s_brow, 64)
            v.tensor_copy(bparts[0], brow).then_inc(s_bsplit, 1)
            dve.wait_ge(s_bsplit, 1)
            v.tensor_tensor(brest, brow, bparts[0], ALU.subtract).then_inc(s_bsplit, 1)
            dve.wait_ge(s_bsplit, 2)
            v.tensor_copy(bparts[1], brest).then_inc(s_bsplit, 1)
            dve.wait_ge(s_bsplit, 3)
            v.tensor_tensor(brow, brest, bparts[1], ALU.subtract).then_inc(s_bsplit, 1)
            dve.wait_ge(s_bsplit, 4)
            v.tensor_copy(bparts[2], brow).then_inc(s_bsplit, 1)
            dve.wait_ge(s_gb, 32)
            v.tensor_scalar(gamma[:], gamma[:], 0.5, None, ALU.mult).then_inc(s_gbh, 1)
            v.tensor_scalar(beta[:], beta[:], 0.5, None, ALU.mult).then_inc(s_gbh, 1)
            v.memset(sofar[:], 0.0).then_inc(s_gbh, 1)
            v.memset(ones16[:], 1.0).then_inc(s_gbh, 1)
            v.memset(oneE[:], 1.0).then_inc(s_gbh, 1)
            dve.wait_ge(s_const, CONST_STEPS)
            dve.wait_ge(s_gbh, 5)

            def chunk_low(n):
                dve.wait_ge(s_whi, n + 1)
                at_ = slice(n % NCH * CH, n % NCH * CH + CH)
                v.scalar_tensor_tensor(w_lo[:, n // NCH, at_], stage[:, n % NCH, :], WW, w_hi[:, n // NCH, at_],
                                       ALU.mult, ALU.subtract).then_inc(s_wlo, 1)

            chain = [0]

            def link(ins):
                chain[0] += 1
                ins.then_inc(s_route, 1)
                dve.wait_ge(s_route, chain[0])

            def wide(small, nt):
                return small.unsqueeze(2).to_broadcast([P, nt, EXPERTS])

            def route_best(n):
                nt = GROUP[n][1]
                w = slice(0, nt)
                link(v.tensor_reduce(m0[:, w], lg[:, w], AX.X, ALU.max))
                link(v.tensor_tensor(same[:, w], lg[:, w], wide(m0[:, w], nt), ALU.is_equal))
                link(v.tensor_tensor(first[:, w], same[:, w], desc[:, w], ALU.mult))
                link(v.tensor_reduce(k0[:, w], first[:, w], AX.X, ALU.max))
                v.tensor_tensor(oh0[:, w], first[:, w], wide(k0[:, w], nt), ALU.is_equal).then_inc(s_oh, 1)

            def route_second(n):
                nt = GROUP[n][1]
                w = slice(0, nt)
                dve.wait_ge(s_oh, 2 * n + 1)
                link(v.scalar_tensor_tensor(lg2[:, w], oh0[:, w], -3.0e38, lg[:, w], ALU.mult, ALU.add))
                link(v.tensor_reduce(m1[:, w], lg2[:, w], AX.X, ALU.max))
                v.tensor_tensor(dm[:, w], m1[:, w], m0[:, w], ALU.subtract).then_inc(s_dm, 1)
                link(v.tensor_tensor(same[:, w], lg2[:, w], wide(m1[:, w], nt), ALU.is_equal))
                link(v.tensor_tensor(first[:, w], same[:, w], desc[:, w], ALU.mult))
                link(v.tensor_reduce(k0[:, w], first[:, w], AX.X, ALU.max))
                v.tensor_tensor(oh1[:, w], first[:, w], wide(k0[:, w], nt), ALU.is_equal).then_inc(s_oh, 1)

            def route_count(n):
                nt = GROUP[n][1]
                dve.wait_ge(s_oh, 2 * n + 2)
                link(v.tensor_tensor(chosen[:, 0:nt], oh0[:, 0:nt], oh1[:, 0:nt], ALU.add))
                for t in range(nt):
                    link(v.tensor_tensor(sofar[:, n % 2, t + 1, :], sofar[:, n % 2, t, :], chosen[:, t, :], ALU.add))
                v.tensor_copy(sofar[:, 1 - n % 2, 0, :], sofar[:, n % 2, nt, :]).then_inc(s_chosen, 1)

            def route_weights(n):
                t0, nt = GROUP[n]
                w = slice(0, nt)
                r = slice(t0 % QR, t0 % QR + nt)
                dve.wait_ge(s_ex, n + 1)
                link(v.tensor_scalar(dm[:, w], ex[:, w], 1.0, None, ALU.add))
                link(v.reciprocal(p0[:, w], dm[:, w]))
                v.tensor_tensor(c0[:, w], oh0[:, w], wide(p0[:, w], nt), ALU.mult)
                link(v.tensor_tensor(p1[:, w], ex[:, w], p0[:, w], ALU.mult))
                link(v.tensor_tensor(c1[:, w], oh1[:, w], wide(p1[:, w], nt), ALU.mult))
                v.tensor_tensor(rows[:, r, COMB:COMB + EXPERTS], c0[:, w], c1[:, w], ALU.add)
                v.tensor_copy(rows[:, r, TOK].bitcast(i32), tokno[:, t0:t0 + nt]).then_inc(s_meta, 1)

            def route_places(n):
                nt = GROUP[n][1]
                w = slice(0, nt)
                if n >= 2:
                    for t in range(*GROUP[n - 2][:1], sum(GROUP[n - 2])):
                        dve.wait_ge(s_sent[t % QR], 16 * TOP * (t // QR + 1))
                dve.wait_ge(s_meta, n + 1)
                dve.wait_ge(s_R, n + 1)
                link(v.tensor_tensor(place[:, w], pR[:, 0:nt * EXPERTS].rearrange("p (t e) -> p t e", e=EXPERTS),
                                     region0[:, w], ALU.add))
                v.tensor_tensor(c0[:, w], place[:, w], oh0[:, w], ALU.mult)
                link(v.tensor_tensor(c1[:, w], place[:, w], oh1[:, w], ALU.mult))
                v.tensor_reduce(slots[:, 0, w], c0[:, w], AX.X, ALU.add)
                link(v.tensor_reduce(slots[:, 1, w], c1[:, w], AX.X, ALU.add))
                v.tensor_copy(slots_i[:, n % 2, :, w], slots[:, :, w]).then_inc(s_slots, 1)

            for i in range(0, STEPS):
                best = routed(i, 10)
                places = routed(i, 11)
                if live(i - 10):
                    dve.wait_ge(s_G, i - 9)
                    n = routed(i - 1, 10)
                    if n is not None:
                        dve.wait_ge(s_R, n + 1)
                    t0 = GROUP[group_of(i - 10)][0]
                    v.tensor_copy(lg[:, i - 10 - t0, :], pG).then_inc(s_lg, 1)
                if places is not None:
                    route_weights(places)
                if live(i - 8):
                    if i - 8 >= PER:
                        dve.wait_ge(s_store[(i - 8) % PER], 16 * ((i - 8) // PER))
                    dve.wait_ge(s_W, i - 7)
                    v.tensor_tensor(x2[:, (i - 8) % PER, :], pW, xall[:, i - 8, :], ALU.add).then_inc(s_x2, 1)
                if places is not None:
                    route_places(places)
                if live(i - 9):
                    dve.wait_ge(s_hi, i - 8)
                    r = (i - 9) % QR
                    v.scalar_tensor_tensor(rows[:, r, LO:LO + E // 2].bitcast(f16), z[:, (i - 9) % 2, :], XW,
                                           rows[:, r, HI:HI + E // 2].bitcast(f16), ALU.mult, ALU.subtract).then_inc(s_lo, 1)
                if live(i - 8):
                    dve.wait_ge(s_x2, i - 7)
                    v.bn_stats(st3[:, i % 2, :], x2[:, (i - 8) % PER, :]).then_inc(s_st3, 1)
                if best is not None:
                    dve.wait_ge(s_lg, i - 9)
                    route_best(best)
                if live(i):
                    dve.wait_ge(s_exp, i + 1)
                    v.tensor_scalar(eq[:, i % 2, :], eq[:, i % 2, :], 1.0, -1.0, ALU.min, ALU.add).then_inc(s_em1, 1)
                if live(i - 8):
                    dve.wait_ge(s_st3, i - 7)
                    v.bn_aggr(mv3[:, i % 2, :], st3[:, i % 2, :]).then_inc(s_mv3, 1)
                if live(i):
                    dve.wait_ge(s_em1, i + 1)
                    v.scalar_tensor_tensor(q[:, i % 2, :], pQ[i % 2], 0.0, eq[:, i % 2, :], ALU.max, ALU.add).then_inc(s_q, 1)
                if best is not None:
                    route_second(best)
                for n in chunks_of(i):
                    chunk_low(n)
                if i % PER == 1 and i // PER + 1 < GROUPS:
                    ln1_stats(i // PER + 1)
                if i % PER == 0 and 0 < i <= TILES:
                    dve.wait_ge(s_KV, i)
                    v.tensor_tensor(kv[:, (i // PER - 1) % 2, :], pKV, headmask[:], ALU.mult).then_inc(s_kv, 1)
                if best is not None:
                    route_count(best)
                if live(i):
                    dve.wait_ge(s_tanh, i + 1)
                    v.scalar_tensor_tensor(vv[:, i % 2, :], th[:, i % 2, 0:E], 1.0, pVU[i % 2][:, 0:E], ALU.add, ALU.mult)\
                     .then_inc(s_v, 1)
                if live(i - 5):
                    dve.wait_ge(s_O, i - 4)
                    v.bn_stats(st2[:, (i - 5) % 2, :], pO).then_inc(s_st2, 1)
                if live(i):
                    v.scalar_tensor_tensor(uring[:, i % 8, :], th[:, i % 2, E:2 * E], 1.0, pVU[i % 2][:, E:2 * E], ALU.add,
                                           ALU.mult).then_inc(s_u, 1)
                if live(i - 5):
                    dve.wait_ge(s_st2, i - 4)
                    v.bn_aggr(mv2[:, (i - 5) % 2, :], st2[:, (i - 5) % 2, :]).then_inc(s_mv2, 1)
                if live(i - 6):
                    dve.wait_ge(s_onb, i - 5)
                    v.tensor_tensor(on[:, i % 2, :], on[:, i % 2, :], uring[:, (i - 6) % 8, :], ALU.mult).then_inc(s_y, 1)
                if live(i - 8):
                    dve.wait_ge(s_rs3, i - 7)
                    v.tensor_scalar(z[:, i % 2, :], x2[:, (i - 8) % PER, :], mv3[:, i % 2, 0:1], rs3[:, i % 2:i % 2 + 1],
                                    ALU.subtract, ALU.mult).then_inc(s_z, 1)

            BE = [P, BLOCKS, EXPERTS]
            dve.wait_ge(s_C, 1)
            link(v.tensor_copy(count[:], pC))
            link(v.tensor_tensor(over, count[:].unsqueeze(2).to_broadcast([P, EXPERTS, TILES]), thresholds[:], ALU.is_gt))
            link(v.tensor_reduce(nblk[:], over, AX.X, ALU.add))
            link(v.tensor_tensor_scan(ends[:], oneE[:], nblk[:], 0.0, ALU.mult, ALU.add))
            link(v.tensor_tensor(past, ends[:].unsqueeze(1).to_broadcast(BE), blockno[:], ALU.is_le))
            link(v.tensor_reduce(bexp, past, AX.X, ALU.add))
            link(v.tensor_tensor(past2, past, nblk[:].unsqueeze(1).to_broadcast(BE), ALU.mult))
            link(v.tensor_reduce(bstart, past2, AX.X, ALU.add))
            link(v.scalar_tensor_tensor(boff, bstart, -float(P), block128[:], ALU.mult, ALU.add))
            link(v.scalar_tensor_tensor(boff, bexp, float(REGION), boff, ALU.mult, ALU.add))
            link(v.tensor_scalar(boff_i[:], boff, float(SPARE), None, ALU.min))
            link(v.tensor_scalar(bexp_i[:], bexp, float(EXPERTS - 1), None, ALU.min))
            link(v.tensor_tensor(padoff_i[:], count[:], region0[:, 0, :], ALU.add))
            dve.sem_inc(s_table, 1)

            def rows_turned(j, par):
                dve.wait_ge(s_XB, j + 1)
                v.tensor_copy(xb[par], pXB).then_inc(s_xb, 1)

            def step(j, slot, head, tail):
                par = slot % 2
                dve.wait_ge(s_sil, j + 1)
                dve.wait_ge(s_H1, j + 1)
                v.scalar_tensor_tensor(inter[par], pH1[par], IW / (XW * WW), sil[par], ALU.mult, ALU.mult)\
                 .then_inc(s_inter, 1)
                if not tail:
                    rows_turned(j + 1, 1 - par)
                if not head:
                    weigh(j - 1, (slot - 1) % SL)
                dve.wait_ge(s_ih, j + 1)
                dve.wait_ge(s_IT, j + 1)
                v.tensor_tensor(il[par].rearrange("p k t -> p (k t)"), pIT, ih[par].rearrange("p k t -> p (k t)"),
                                ALU.subtract).then_inc(s_il, 1)

            def weigh(j, slot):
                e = dve.value_load(bexp_i[0:1, bass.ds(j, 1)], min_val=0, max_val=EXPERTS - 1)
                dve.wait_ge(s_Y, j + 1)
                v.tensor_scalar(ys[slot], pY[slot % 2], blk[slot][:, bass.ds(COMB + e, 1)], 1.0 / (IW * WW),
                                ALU.mult, ALU.mult).then_inc(s_ys, 1)
            rows_turned(0, 0)
            step(0, 0, True, False)
            with dve.Fori(0, (BLOCKS - 3) // SL) as k:
                for r in range(SL):
                    step(SL * k + 1 + r, (1 + r) % SL, False, False)
            step(BLOCKS - 2, (BLOCKS - 2) % SL, False, False)
            step(BLOCKS - 1, (BLOCKS - 1) % SL, False, True)
            weigh(BLOCKS - 1, (BLOCKS - 1) % SL)

        @block.tensor
        def _(pe):
            m = nc.tensor
            pe.wait_ge(s_const, CONST_STEPS)
            pe.wait_ge(s_gbh, 5)

            def turn(dst, src, done):
                for k in range(KT):
                    mm = m.transpose(dst[:, k * P:(k + 1) * P], src[:, k * P:(k + 1) * P], ident[:])
                mm.then_inc(done, 1)

            def project(dst, lhs, w, c0_, n, done):
                m.matmul(dst, ones16[0:3, :], bias3[:, c0_:c0_ + n], start=True, stop=False)
                for k in range(KT):
                    mm = m.matmul(dst, lhs[:, k, :], w[:, k, :], start=False, stop=(k == KT - 1))
                mm.then_inc(done, 1)

            for i in range(FIRST_STEP, STEPS):
                if live(i):
                    pe.wait_ge(s_xT, i + 1)
                    if i == 0:
                        pe.wait_ge(s_wA, 80)
                        pe.wait_ge(s_bias3, 48)
                    project(pQ[i % 2], xT[:, i % 2], wcat[:, :, 0:E], 0, E, s_Q)
                    if i >= 2:
                        pe.wait_ge(s_u, i - 1)
                    project(pVU[i % 2], xT[:, i % 2], wcat[:, :, E:3 * E], E, 2 * E, s_VU)
                if live(i - 7):
                    pe.wait_ge(s_y, i - 6)
                    if live(i - 8):
                        pe.wait_ge(s_x2, i - 7)
                    turn(pYT, on[:, (i - 7) % 2, :], s_YT)
                if live(i - 1):
                    j = i - 1
                    pe.wait_ge(s_q, i)
                    pe.wait_ge(s_v, i)
                    if j % PER == 0 and j > 0:
                        pe.wait_ge(s_kv, j // PER)
                    for k in range(KT):
                        kc = slice(k * P, (k + 1) * P)
                        mm = m.matmul(pKV[:, kc], q[:, j % 2, kc], vv[:, j % 2, kc], start=(j % PER == 0 and k == 0),
                                      stop=(j % PER == PER - 1), skip_group_check=True)
                    mm.then_inc(s_KV, 1)
                    turn(pQT[j % 2], q[:, j % 2, :], s_QT)
                if live(i - 5):
                    j = i - 5
                    pe.wait_ge(s_kv, j // PER + 1)
                    pe.wait_ge(s_qT, j + 1)
                    if j >= 1:
                        pe.wait_ge(s_on, j)
                    for k in range(KT):
                        kc = slice(k * P, (k + 1) * P)
                        mm = m.matmul(pO[:, kc], qT[:, j % QR, kc], kv[:, j // PER % 2, kc], start=True, stop=True)
                    mm.then_inc(s_O, 1)
                if live(i - 7):
                    pe.wait_ge(s_yT, i - 6)
                    project(pW, yT[:].rearrange("p (k t) -> p k t", t=P), wout, 3 * E, E, s_W)
                if live(i - 9):
                    pe.wait_ge(s_z, i - 8)
                    if live(i - 10):
                        pe.wait_ge(s_lg, i - 9)
                    n = routed(i - 1, 10)
                    if n is not None:
                        pe.wait_ge(s_slots, n + 1)
                    turn(pZT, z[:, (i - 9) % 2, :], s_ZT)
                if live(i + 1):
                    pe.wait_ge(s_xn, i + 2)
                    if live(i - 1):
                        pe.wait_ge(s_qT, i)
                    turn(pXT[(i + 1) % 2], xn[:, (i + 1) % 2, :], s_XT)
                if live(i - 9):
                    pe.wait_ge(s_zT, i - 8)
                    for k in range(KT):
                        mm = m.matmul(pG, zT[:, k * P:(k + 1) * P], gatew[:, k, :], start=(k == 0), stop=(k == KT - 1))
                    mm.then_inc(s_G, 1)
                n = routed(i, 10)
                if n is not None:
                    nt = GROUP[n][1]
                    pe.wait_ge(s_chosen, n + 1)
                    m.matmul(pR[:, 0:nt * EXPERTS], before[:], chosen[:, 0:nt].rearrange("p t e -> p (t e)"),
                             start=True, stop=False)
                    m.matmul(pR[:, 0:nt * EXPERTS], ones16[:], sofar[:, n % 2, 0:nt, :].rearrange("p t e -> p (t e)"),
                             start=False, stop=True).then_inc(s_R, 1)
            m.matmul(pC, ones16[:], sofar[:, len(GROUP) % 2, 0, :], start=True, stop=True).then_inc(s_C, 1)

            def turn_rows(j, slot, uses):
                pe.wait_ge(s_blk[slot], 16 * uses)
                r16 = blk[slot][:, 0:E].bitcast(f16)
                for k in range(2 * KT):
                    mm = m.transpose(pXB[:, k, :], r16[:, k * P:(k + 1) * P], ident16[:])
                mm.then_inc(s_XB, 1)

            def three(dst, pairs, done):
                last = len(pairs) * 3 - 1
                n = 0
                for hi, lo_, wh, wl in pairs:
                    for l, r in ((hi, wh), (hi, wl), (lo_, wh)):
                        mm = m.matmul(dst, l, r, start=(n == 0), stop=(n == last))
                        n += 1
                mm.then_inc(done, 1)

            def up(j, slot, e):
                par = slot % 2
                pe.wait_ge(s_xb, j + 1)
                for c, dst, done in ((0, pH0[par], s_H0), (1, pH1[par], s_H1)):
                    three(dst, [(xb[par][:, k, :], xb[par][:, KT + k, :],
                                 weights_of(w_hi, e, c * CH + k * MLP, MLP), weights_of(w_lo, e, c * CH + k * MLP, MLP))
                                for k in range(KT)], done)

            def turn_inter(j, slot):
                par = slot % 2
                pe.wait_ge(s_inter, j + 1)
                for k in range(MT):
                    mm = m.transpose(pIT[:, k * P:(k + 1) * P], inter[par][:, k * P:(k + 1) * P], ident[:])
                mm.then_inc(s_IT, 1)

            def down(j, slot):
                par = slot % 2
                e = pe.value_load(bexp_i[0:1, bass.ds(j, 1)], min_val=0, max_val=EXPERTS - 1)
                pe.wait_ge(s_il, j + 1)
                three(pY[par], [(ih[par][:, k, :], il[par][:, k, :], weights_of(w_hi, e, 2 * CH + k * E, E),
                                 weights_of(w_lo, e, 2 * CH + k * E, E)) for k in range(MT)], s_Y)

            def step(j, slot, uses, head, tail):
                e = pe.value_load(bexp_i[0:1, bass.ds(j, 1)], min_val=0, max_val=EXPERTS - 1)
                up(j, slot, e)
                if not tail:
                    turn_rows(j + 1, (slot + 1) % SL, uses)
                if not head:
                    down(j - 1, (slot - 1) % SL)
                turn_inter(j, slot)
            pe.wait_ge(s_table, 1)
            pe.wait_ge(s_wlo, NCH * EXPERTS)
            turn_rows(0, 0, 1)
            step(0, 0, 1, True, False)
            with pe.Fori(0, (BLOCKS - 3) // SL) as k:
                for r in range(SL):
                    step(SL * k + 1 + r, (1 + r) % SL, k + (r + 2) // SL + 1, False, False)
            step(BLOCKS - 2, (BLOCKS - 2) % SL, (BLOCKS - 1) // SL + 1, False, False)
            step(BLOCKS - 1, (BLOCKS - 1) % SL, 0, False, True)
            down(BLOCKS - 1, (BLOCKS - 1) % SL)


_INS = ['x', 'Wqk', 'bqk', 'Wv', 'bv', 'Wu', 'bu', 'Wo', 'bo', 'ln_g', 'ln_b']
_FFN = ['gate_kernel', 'w0_kernel', 'w1_kernel', 'wo_kernel']


def kernel(**inputs):
    import numpy as _np
    import concourse.bacc as _bacc
    from concourse import mybir as _mybir
    from concourse.bass_utils import run_bass_kernel_spmd as _run

    nc = _bacc.Bacc("TRN2", target_bir_lowering=False, num_devices=1)
    arrays, args = {}, []
    for name in ['L0_attn_' + n for n in _INS] + ['L0_ffn_' + n for n in _FFN]:
        a = _np.ascontiguousarray(inputs[name])
        if name == 'L0_attn_x':
            batch, seq, width = a.shape
            a = a.reshape(batch * seq, width)
        arrays["in_" + name] = a
        args.append(nc.dram_tensor("in_" + name, a.shape, _mybir.dt.from_np(a.dtype), kind="ExternalInput").ap())
    out = nc.dram_tensor("out_0", (batch * seq + 128, width), _mybir.dt.float32, kind="ExternalOutput").ap()
    linear_attention_then_top2_moe(nc, *args, out)
    r = _run(nc, [arrays], core_ids=[0])
    return r.results[0]["out_0"][:batch * seq].reshape(batch, seq, width)
```

```python
import concourse.bass as bass
from concourse import mybir
from contextlib import ExitStack


def linear_attention_then_top2_moe(nc, x, Wqk, bqk, Wv, bv, Wu, bu, Wo, bo, ln_g, ln_b, gate, w0, w1, wo, out):
    f32, f16, bf16, i32 = mybir.dt.float32, mybir.dt.float16, mybir.dt.bfloat16, mybir.dt.int32
    ALU, ACT, AX = mybir.AluOpType, mybir.ActivationFunctionType, mybir.AxisListType

    P = 128
    T, E = x.shape
    EXPERTS, _, MLP = w0.shape
    TILES = T // P
    PER = 4
    GROUPS = TILES // PER
    DH = 16
    KT = E // P
    MT = MLP // P
    EPS = 1e-5
    TOP = 2
    REGION = T + P
    SPARE = EXPERTS * REGION
    BLOCKS = (TOP * T + EXPERTS * (P - 1)) // P
    XW, WW, IW = 256.0, 256.0, 64.0

    HI, LO, COMB, TOK, ROW = 0, E // 2, E, E + EXPERTS, E + 16
    CH = 1024
    NCH = 3
    EW = NCH * CH

    sent = nc.dram_tensor("sent", (SPARE + P, ROW), f32).ap()

    ctx = ExitStack()
    with ctx:
        def sb(name, shape, dt):
            return ctx.enter_context(nc.sbuf_tensor(name, shape, dt))

        def pb(name, shape, dt):
            return ctx.enter_context(nc.psum_tensor(name, shape, dt))

        def sem(name):
            return ctx.enter_context(nc.semaphore(name))

        ident = sb("ident", [P, P], f32)
        ident16 = sb("ident16", [P, P], f16)
        before = sb("before", [P, P], bf16)
        ones16 = sb("ones16", [P, P], bf16)
        headmask = sb("headmask", [P, KT * P], f32)
        neghalf = sb("neghalf", [P, TILES], f32)
        desc = sb("desc", [P, PER, EXPERTS], f32)
        region0 = sb("region0", [P, PER, EXPERTS], f32)
        thresholds = sb("thresholds", [P, EXPERTS, TILES], f32)
        blockno = sb("blockno", [P, BLOCKS, EXPERTS], f32)
        block128 = sb("block128", [P, BLOCKS], f32)
        oneE = sb("oneE", [P, EXPERTS], f32)
        tokno = sb("tokno", [P, TILES], i32)
        padrows = sb("padrows", [P, ROW], f32)
        gamma = sb("gamma", [P, KT], f32)
        beta = sb("beta", [P, KT], f32)
        warm = sb("warm", [P, 1], f32)
        wcat = sb("wcat", [P, KT, 3 * E], f32)
        wout = sb("wout", [P, KT, E], f32)
        gatew = sb("gatew", [P, KT, EXPERTS], f32)
        bias3 = sb("bias3", [3, 4 * E], bf16)
        BC = 4 * E // P
        bcol = sb("bcol", [P, BC], f32)
        brest = sb("brest", [P, BC], f32)
        bparts = sb("bparts", [P, 3, BC], bf16)
        stage = sb("stage", [P, NCH, CH], f32)
        w_hi = sb("w_hi", [P, EXPERTS, EW], f16)
        w_lo = sb("w_lo", [P, EXPERTS, EW], f16)
        room = sb("room", [P, 2 * TILES * E], f32)
        xall = room[:, 0:TILES * E].rearrange("p (t e) -> p t e", e=E)
        uring = room[:, TILES * E:TILES * E + 8 * E].rearrange("p (t e) -> p t e", e=E)
        st1 = sb("st1", [P, TILES, 6], f32)
        mv1 = sb("mv1", [P, TILES, 2], f32)
        ve1 = sb("ve1", [P, TILES], f32)
        rs1 = sb("rs1", [P, TILES], f32)
        nm1 = sb("nm1", [P, TILES], f32)
        xn = sb("xn", [P, 2, E], f32)
        xT = sb("xT", [P, 2, KT, P], f32)
        eq = sb("eq", [P, 2, E], f32)
        th = sb("th", [P, 2, 2 * E], f32)
        q = sb("q", [P, 2, E], f32)
        vv = sb("vv", [P, 2, E], f32)
        QR = 8
        qT = sb("qT", [P, QR, KT * P], f32)
        kv = sb("kv", [P, 2, KT * P], f32)
        st2 = sb("st2", [P, QR, 6], f32)
        mv2 = sb("mv2", [P, QR, 2], f32)
        ve2 = sb("ve2", [P, QR], f32)
        rs2 = sb("rs2", [P, QR], f32)
        nm2 = sb("nm2", [P, QR], f32)
        on = sb("on", [P, 2, E], f32)
        onT = sb("onT", [P, KT * P], f32)
        yT = sb("yT", [P, 2, KT * P], f32)
        x2 = sb("x2", [P, PER, E], f32)
        st3 = sb("st3", [P, 2, 6], f32)
        mv3 = sb("mv3", [P, 2, 2], f32)
        ve3 = sb("ve3", [P, 2], f32)
        rs3 = sb("rs3", [P, 2], f32)
        z = sb("z", [P, 2, E], f32)
        zT = sb("zT", [P, KT * P], f32)
        rows = sb("rows", [P, QR, ROW], f32)
        lg = sb("lg", [P, PER, EXPERTS], f32)
        lg2 = sb("lg2", [P, PER, EXPERTS], f32)
        same = sb("same", [P, PER, EXPERTS], f32)
        first = sb("first", [P, PER, EXPERTS], f32)
        oh0 = sb("oh0", [P, PER, EXPERTS], f32)
        oh1 = sb("oh1", [P, PER, EXPERTS], f32)
        c0 = sb("c0", [P, PER, EXPERTS], f32)
        c1 = sb("c1", [P, PER, EXPERTS], f32)
        chosen = sb("chosen", [P, 2, PER, EXPERTS], bf16)
        sofar = sb("sofar", [P, 2, EXPERTS], bf16)
        inside = sb("inside", [P, EXPERTS], bf16)
        m0 = sb("m0", [P, PER], f32)
        m1 = sb("m1", [P, PER], f32)
        k0 = sb("k0", [P, PER], f32)
        dm = sb("dm", [P, PER], f32)
        ex = sb("ex", [P, PER], f32)
        p0 = sb("p0", [P, PER], f32)
        p1 = sb("p1", [P, PER], f32)
        h0 = sb("h0", [P, PER, EXPERTS], f32)
        h1 = sb("h1", [P, PER, EXPERTS], f32)
        place = sb("place", [P, PER, EXPERTS], f32)
        slots = sb("slots", [P, TOP, PER], f32)
        slots_i = sb("slots_i", [P, 3, TOP, PER], i32)
        count = sb("count", [P, EXPERTS], f32)
        nblk = sb("nblk", [P, EXPERTS], f32)
        ends = sb("ends", [P, EXPERTS], f32)
        bexp_i = sb("bexp_i", [P, BLOCKS], i32)
        boff_i = sb("boff_i", [P, BLOCKS], i32)
        padoff_i = sb("padoff_i", [P, EXPERTS], i32)
        at = [0]

        def cut(words):
            at[0] += words
            return room[:, at[0] - words:at[0]]
        SL = 4
        blk = [cut(ROW) for _ in range(SL)]
        sil = [cut(MLP) for _ in range(2)]
        inter = [cut(MLP) for _ in range(2)]
        xb = [cut(2 * KT * P // 2).bitcast(f16).rearrange("p (k t) -> p k t", t=P) for _ in range(2)]
        ih = [cut(MLP // 2).bitcast(f16).rearrange("p (k t) -> p k t", t=P) for _ in range(2)]
        il = [cut(MLP // 2).bitcast(f16).rearrange("p (k t) -> p k t", t=P) for _ in range(2)]
        ys = [cut(E) for _ in range(SL)]
        over = cut(EXPERTS * TILES).rearrange("p (e t) -> p e t", t=TILES)
        past = cut(BLOCKS * EXPERTS).rearrange("p (j e) -> p j e", e=EXPERTS)
        past2 = cut(BLOCKS * EXPERTS).rearrange("p (j e) -> p j e", e=EXPERTS)
        bexp = cut(BLOCKS)
        bstart = cut(BLOCKS)
        boff = cut(BLOCKS)
        assert at[0] <= 2 * TILES * E

        bank = [pb(f"bank{n}", [P, 512], f32) for n in range(8)]
        pVU = [bank[0][:, :], bank[1][:, :]]
        pQ = [bank[2][:, 0:E], bank[3][:, 0:E]]
        pXT = [bank[2][:, E:2 * E], bank[3][:, E:2 * E]]
        pKV = bank[4][:, 0:KT * P]
        pQT = pXT
        pO = [bank[5][:, 0:E]] * (TILES - PER) + [bank[n][:, 0:E] for n in range(PER)]
        pYT = bank[5][:, E:2 * E]
        pW = bank[6][:, 0:E]
        pZT = bank[7][:, 0:E]
        pG = bank[7][:, E:E + EXPERTS]
        pR = [bank[6][:, E:E + PER * EXPERTS]] + [bank[4][:, E:E + PER * EXPERTS]] * 4
        pC = bank[4][:, 400:400 + EXPERTS]
        pH0 = [bank[0][:, :], bank[2][:, :]]
        pH1 = [bank[1][:, :], bank[3][:, :]]
        pXB = bank[4][:, 0:KT * P].bitcast(f16).rearrange("p (k t) -> p k t", t=P)
        pIT = bank[5][:, :]
        pY = [bank[6][:, 0:E], bank[7][:, 0:E]]

        s_const = sem("s_const")
        s_xin = [sem(f"s_xin{g}") for g in range(GROUPS)]
        s_wA = sem("s_wA")
        s_wB = sem("s_wB")
        s_brow = sem("s_brow")
        s_warm = sem("s_warm")
        s_fill = sem("s_fill")
        s_bsplit = sem("s_bsplit")
        s_bias3 = sem("s_bias3")
        s_gb = sem("s_gb")
        s_gbh = sem("s_gbh")
        s_stage = [sem(f"s_stage{n}") for n in range(NCH)]
        s_whi = sem("s_whi")
        s_wlo = sem("s_wlo")
        s_st1 = sem("s_st1")
        s_mv1 = sem("s_mv1")
        s_ve1 = sem("s_ve1")
        s_rs1 = sem("s_rs1")
        s_xn = sem("s_xn")
        s_XT = sem("s_XT")
        s_xT = sem("s_xT")
        s_Q = sem("s_Q")
        s_V = sem("s_V")
        s_VU = sem("s_VU")
        s_exp = sem("s_exp")
        s_tanh = sem("s_tanh")
        s_em1 = sem("s_em1")
        s_q = sem("s_q")
        s_v = sem("s_v")
        s_u = sem("s_u")
        s_KV = sem("s_KV")
        s_QT = sem("s_QT")
        s_qT = sem("s_qT")
        s_kv = sem("s_kv")
        s_O = sem("s_O")
        s_st2 = sem("s_st2")
        s_mv2 = sem("s_mv2")
        s_ve2 = sem("s_ve2")
        s_rs2 = sem("s_rs2")
        s_nm2 = sem("s_nm2")
        s_on = sem("s_on")
        s_onT = sem("s_onT")
        s_y = sem("s_y")
        s_YT = sem("s_YT")
        s_W = sem("s_W")
        s_x2 = sem("s_x2")
        s_st3 = sem("s_st3")
        s_mv3 = sem("s_mv3")
        s_ve3 = sem("s_ve3")
        s_rs3 = sem("s_rs3")
        s_z = sem("s_z")
        s_hi = sem("s_hi")
        s_lo = sem("s_lo")
        s_ZT = sem("s_ZT")
        s_zT = sem("s_zT")
        s_G = sem("s_G")
        s_lg = sem("s_lg")
        s_route = sem("s_route")
        s_oh = sem("s_oh")
        s_dm = sem("s_dm")
        s_ex = sem("s_ex")
        s_chosen = sem("s_chosen")
        s_sofar = sem("s_sofar")
        s_place = sem("s_place")
        s_R = sem("s_R")
        s_slots = sem("s_slots")
        s_sent = [sem(f"s_sent{n}") for n in range(QR)]
        s_store = [sem(f"s_store{n}") for n in range(PER)]
        s_spare = sem("s_spare")
        s_C = sem("s_C")
        s_padoff = sem("s_padoff")
        s_table = sem("s_table")
        s_padA = sem("s_padA")
        s_padS = sem("s_padS")
        s_blk = [sem(f"s_blk{n}") for n in range(SL)]
        s_XB = sem("s_XB")
        s_xb = sem("s_xb")
        s_H0 = sem("s_H0")
        s_H1 = sem("s_H1")
        s_sil = sem("s_sil")
        s_inter = sem("s_inter")
        s_IT = sem("s_IT")
        s_ih = sem("s_ih")
        s_il = sem("s_il")
        s_Y = sem("s_Y")
        s_ys = sem("s_ys")
        s_added = sem("s_added")

        block = ctx.enter_context(nc.Block())

        CONST_STEPS = 19

        def weights_of(part, e, c0_, n):
            return part[:, bass.ds(e, 1), c0_:c0_ + n].rearrange("p a n -> p (a n)")

        def chunk_source(e, c):
            return (w0, w1, wo)[c][e, :, :].rearrange("(k p) n -> p k n", p=P)

        def chunk_view(c):
            w = MLP if c < 2 else E
            return stage[:, c, :].rearrange("p (k n) -> p k n", n=w)

        GROUP = [(0, 4), (4, 4), (8, 4), (12, 4)]
        FIRST_STEP, STEPS = -1, TILES + 13
        NCHUNK = NCH * EXPERTS

        def live(i):
            return 0 <= i < TILES

        def chunks_of(i):
            each = [2] + [1] * 2 + [2, 1] * 3 + [1] * 4 + [0] * 2 + [1] * 7
            assert sum(each) == NCHUNK
            return range(sum(each[:i + 1]), sum(each[:i + 2]))

        def stats_of(i):
            j = i - 5
            return [j] if 0 <= j < TILES - PER else list(range(j, TILES)) if j == TILES - PER else []

        def routed(i, lag):
            for n, (t0, nt) in enumerate(GROUP):
                if t0 + nt - 1 == i - lag:
                    return n
            return None

        def group_of(tile):
            return max(n for n, (t0, _) in enumerate(GROUP) if t0 <= tile)

        @block.sync
        def _(sp):
            def load_x(g):
                sp.dma_start(xall[:, PER * g:PER * g + PER, :],
                             x[P * PER * g:P * PER * (g + 1), :].rearrange("(t p) e -> p t e", p=P)).then_inc(s_xin[g], 16)
            def load_stage(n):
                sp.dma_start(chunk_view(n), chunk_source(0, n)).then_inc(s_stage[n], 16)

            load_x(0)
            for n, src in enumerate((bqk, bv, bu, bo)):
                sp.dma_start(bcol[n * E // BC:(n + 1) * E // BC, :], src.rearrange("(p c) -> p c", c=BC)).then_inc(s_brow, 16)
            load_stage(0)
            sp.wait_ge(s_bsplit, 5)
            for n in range(3):
                sp.dma_start(bias3[n:n + 1, :], bparts[:, n, :]).then_inc(s_bias3, 16)
            load_x(1)
            load_stage(1)
            load_stage(2)
            for g in range(2, GROUPS):
                load_x(g)
            for i in range(FIRST_STEP, STEPS):
                for n in chunks_of(i):
                    if n + NCH < NCHUNK:
                        sp.wait_ge(s_wlo, n + 1)
                        sp.dma_start(chunk_view(n % NCH), chunk_source((n + NCH) // NCH, n % NCH))\
                          .then_inc(s_stage[n % NCH], 16)
                if i == 2:
                    sp.wait_ge(s_const, CONST_STEPS)
                    sp.dma_start(sent[SPARE:SPARE + P, :], padrows[:, :]).then_inc(s_spare, 16)
                    sp.dma_start(out[T:T + P, :], padrows[:, 0:E]).then_inc(s_spare, 16)
                if live(i - 8):
                    sp.wait_ge(s_x2, i - 7)
                    sp.dma_start(out[(i - 8) * P:(i - 7) * P, :], x2[:, (i - 8) % PER, :]).then_inc(s_store[(i - 8) % PER], 16)
            sp.wait_ge(s_padoff, 1)
            for e in range(EXPERTS // 2, EXPERTS):
                off = sp.value_load(padoff_i[0:1, e:e + 1], min_val=0, max_val=SPARE - P)
                sp.dma_start(sent[bass.ds(off, P), :], padrows[:, :]).then_inc(s_padS, 16)
            sp.wait_ge(s_table, 1)
            sp.wait_ge(s_padS, 16 * (EXPERTS // 2))
            sp.wait_ge(s_padA, 16 * (EXPERTS // 2))
            sp.wait_ge(s_spare, 32)
            for n in range(QR):
                sp.wait_ge(s_sent[n], 16 * TOP * TILES // QR)

            def load(j, slot):
                off = sp.value_load(boff_i[0:1, bass.ds(j, 1)], min_val=0, max_val=SPARE)
                sp.dma_start(blk[slot], sent[bass.ds(off, P), :]).then_inc(s_blk[slot], 16)
            for j in range(SL):
                load(j, j)
            with sp.Fori(0, (BLOCKS - SL) // SL) as k:
                for r in range(SL):
                    sp.wait_ge(s_added, 16 * (SL * k + r + 1))
                    load(SL * k + SL + r, r)
            for j in range(BLOCKS - (BLOCKS - SL) % SL, BLOCKS):
                sp.wait_ge(s_added, 16 * (j - SL + 1))
                load(j, j % SL)
            sp.wait_ge(s_added, 16 * BLOCKS)

        @block.gpsimd
        def _(pool):
            g = nc.gpsimd
            g.memset(ident[:], 0.0).then_inc(s_const, 1)
            g.memset(ident16[:], 0.0).then_inc(s_const, 1)
            g.memset(before[:], 1.0).then_inc(s_const, 1)
            g.memset(headmask[:], 0.5).then_inc(s_const, 1)
            g.memset(neghalf[:], -0.5).then_inc(s_const, 1)
            pool.wait_ge(s_const, 5)
            g.affine_select(out=ident[:], in_=ident[:], compare_op=ALU.not_equal, fill=1.0, base=0,
                            pattern=[[-1, P]], channel_multiplier=1).then_inc(s_const, 1)
            g.affine_select(out=ident16[:], in_=ident16[:], compare_op=ALU.not_equal, fill=1.0, base=0,
                            pattern=[[-1, P]], channel_multiplier=1).then_inc(s_const, 1)
            g.affine_select(out=before[:], in_=before[:], compare_op=ALU.is_gt, fill=0.0, base=0,
                            pattern=[[1, P]], channel_multiplier=-1).then_inc(s_const, 1)
            hm = headmask[:].rearrange("p (k a c) -> p k a c", k=KT, c=DH)
            g.affine_select(out=hm, in_=hm, compare_op=ALU.is_ge, fill=0.0, base=0,
                            pattern=[[0, KT], [-DH, P // DH], [0, DH]], channel_multiplier=1).then_inc(s_const, 1)

            def ln1_scale(n):
                at_ = slice(PER * n, PER * n + PER)
                pool.wait_ge(s_ve1, n + 1)
                g.tensor_tensor(rs1[:, at_], ve1[:, at_], neghalf[:, 0:PER], ALU.pow).then_inc(s_rs1, 1)
                pool.wait_ge(s_rs1, 3 * n + 1)
                g.tensor_tensor(nm1[:, at_], mv1[:, at_, 0], rs1[:, at_], ALU.mult).then_inc(s_rs1, 1)
                pool.wait_ge(s_rs1, 3 * n + 2)
                g.tensor_scalar(nm1[:, at_], nm1[:, at_], -1.0, 1.0, ALU.mult, ALU.mult).then_inc(s_rs1, 1)
            ln1_scale(0)
            pool.wait_ge(s_const, 9)
            g.affine_select(out=hm, in_=hm, compare_op=ALU.is_ge, fill=0.0, base=DH - 1,
                            pattern=[[0, KT], [DH, P // DH], [0, DH]], channel_multiplier=-1).then_inc(s_const, 1)
            g.iota(desc[:], [[0, PER], [-1, EXPERTS]], base=EXPERTS, channel_multiplier=0,
                   allow_small_or_imprecise_dtypes=True).then_inc(s_const, 1)
            g.iota(region0[:], [[0, PER], [REGION, EXPERTS]], base=0, channel_multiplier=0,
                   allow_small_or_imprecise_dtypes=True).then_inc(s_const, 1)
            g.iota(thresholds[:], [[0, EXPERTS], [P, TILES]], base=0, channel_multiplier=0,
                   allow_small_or_imprecise_dtypes=True).then_inc(s_const, 1)
            g.iota(blockno[:], [[1, BLOCKS], [0, EXPERTS]], base=0, channel_multiplier=0,
                   allow_small_or_imprecise_dtypes=True).then_inc(s_const, 1)
            g.iota(block128[:], [[P, BLOCKS]], base=0, channel_multiplier=0,
                   allow_small_or_imprecise_dtypes=True).then_inc(s_const, 1)
            g.iota(tokno[:], [[P, TILES]], base=0, channel_multiplier=1).then_inc(s_const, 1)
            g.memset(padrows[:], 0.0).then_inc(s_const, 1)
            pool.wait_ge(s_const, 17)
            g.iota(padrows[:, TOK:TOK + 1].bitcast(i32), [[0, 1]], base=T, channel_multiplier=1).then_inc(s_const, 1)
            g.memset(rows[:, :, TOK + 1:ROW], 0.0).then_inc(s_const, 1)
            g.dma_start(wout[:], Wo.rearrange("(k p) n -> p k n", p=P)).then_inc(s_wB, 16)
            g.dma_start(gatew[:], gate.rearrange("(k p) n -> p k n", p=P)).then_inc(s_wB, 16)
            for k in range(KT):
                for dst, src in ((gamma, ln_g), (beta, ln_b)):
                    g.dma_start(dst[:, k:k + 1], src[k * P:(k + 1) * P].rearrange("(p a) -> p a", a=1)).then_inc(s_gb, 16)
            ln1_scale(1)

            def send(i, c):
                for n, (t0, nt) in enumerate(GROUP):
                    per = 1 if t0 < 2 * PER else 2
                    first = per * (i - (t0 + nt + 11))
                    if 0 <= first < nt:
                        pool.wait_ge(s_slots, n + 1)
                        for k in range(first, first + per):
                            g.indirect_dma_start(sent, bass.IndirectOffsetOnAxis(slots_i[:, n % 3, c, k:k + 1], 0),
                                                 rows[:, (t0 + k) % QR, :], None).then_inc(s_sent[(t0 + k) % QR], 16)

            def scale(js):
                w, n = slice(js[0] % QR, js[0] % QR + len(js)), len(js)
                pool.wait_ge(s_mv2, js[-1] + 1)
                g.tensor_scalar(ve2[:, w], mv2[:, w, 1], 1.0, EPS, ALU.mult, ALU.add).then_inc(s_ve2, n)
                pool.wait_ge(s_ve2, js[-1] + 1)
                g.tensor_tensor(rs2[:, w], ve2[:, w], neghalf[:, 0:n], ALU.pow).then_inc(s_rs2, n)
                pool.wait_ge(s_rs2, js[-1] + 1)
                if n == 1:
                    g.tensor_scalar(nm2[:, w], mv2[:, w, 0], rs2[:, w], -1.0, ALU.mult, ALU.mult).then_inc(s_nm2, 1)
                else:
                    g.tensor_tensor(ve2[:, w], mv2[:, w, 0], rs2[:, w], ALU.mult).then_inc(s_ve2, n)
                    pool.wait_ge(s_ve2, js[-1] + 1 + n)
                    g.tensor_scalar(nm2[:, w], ve2[:, w], -1.0, 1.0, ALU.mult, ALU.mult).then_inc(s_nm2, n)

            for i in range(0, STEPS):
                if i in (1, 3):
                    ln1_scale((i + 3) // 2)
                if stats_of(i - 1) and i - 1 <= TILES:
                    scale(stats_of(i - 1))
                if live(i - 8):
                    n = (i - 8) % 2
                    pool.wait_ge(s_mv3, i - 7)
                    g.tensor_scalar(ve3[:, n:n + 1], mv3[:, n, 1:2], 1.0, EPS, ALU.mult, ALU.add).then_inc(s_ve3, 1)
                    pool.wait_ge(s_ve3, i - 7)
                    g.tensor_tensor(rs3[:, n:n + 1], ve3[:, n:n + 1], neghalf[:, 0:1], ALU.pow).then_inc(s_rs3, 1)
                if i == TILES + 1:
                    scale(stats_of(i))
                send(i, 0)
                send(i, 1)

            for n in range(PER):
                pool.wait_ge(s_store[n], 16 * TILES // PER)
            pool.wait_ge(s_spare, 32)

            def add_block(j, slot, head):
                pool.wait_ge(s_ys, j + 1)
                if not head:
                    pool.wait_ge(s_added, 16 * j)
                pool.nop(nofuse=True)
                g.indirect_dma_start(out, bass.IndirectOffsetOnAxis(blk[slot][:, TOK:TOK + 1].bitcast(i32), 0),
                                     ys[slot], None, compute_op=ALU.add).then_inc(s_added, 16)
            add_block(0, 0, True)
            with pool.Fori(0, (BLOCKS - 3) // SL) as k:
                for r in range(SL):
                    add_block(SL * k + 1 + r, (1 + r) % SL, False)
            for j in range(BLOCKS - 2, BLOCKS):
                add_block(j, j % SL, False)

        @block.scalar
        def _(act):
            a = nc.scalar
            for src, lo_ in ((Wqk, 0), (Wv, E), (Wu, 2 * E)):
                act.dma_start(wcat[:, :, lo_:lo_ + E], src.rearrange("(k p) n -> p k n", p=P)).then_inc(s_wA, 16)

            act.wait_ge(s_const, 5)
            a.activation(warm[:], neghalf[:, 0:1], ACT.Exp).then_inc(s_warm, 1)

            def chunk_high(n):
                act.wait_ge(s_stage[n % NCH], 16 * (n // NCH + 1))
                a.activation(w_hi[:, n // NCH, n % NCH * CH:n % NCH * CH + CH], stage[:, n % NCH, :], ACT.Copy,
                             scale=WW).then_inc(s_whi, 1)

            def normalise(i):
                if live(i - 6):
                    j = i - 6
                    act.wait_ge(s_nm2, j + 1)
                    a.activation(on[:, i % 2, :], pO[j], ACT.Identity, scale=rs2[:, j % QR:j % QR + 1],
                                 bias=nm2[:, j % QR:j % QR + 1]).then_inc(s_on, 1)

            def widen(i):
                if live(i - 6):
                    if i == 6:
                        act.wait_ge(s_gbh, 2)
                    else:
                        act.wait_ge(s_y, i - 6)
                    act.wait_ge(s_YT, i - 5)
                    for k in range(KT):
                        a.activation(onT[:, k * P:(k + 1) * P], pYT[:, k * P:(k + 1) * P], ACT.Identity,
                                     scale=gamma[:, k:k + 1], bias=beta[:, k:k + 1]).then_inc(s_onT, 1)

            def evacuate_z(i):
                if live(i - 9):
                    act.wait_ge(s_ZT, i - 8)
                    a.activation(zT[:], pZT, ACT.Copy).then_inc(s_zT, 1)
                n = routed(i, 11)
                if n is not None:
                    act.wait_ge(s_dm, n + 1)
                    a.activation(ex[:, 0:GROUP[n][1]], dm[:, 0:GROUP[n][1]], ACT.Exp).then_inc(s_ex, 1)

            for i in range(FIRST_STEP, STEPS):
                if i > TILES + 1:
                    normalise(i)
                if live(i - 9):
                    if i - 9 >= QR:
                        act.wait_ge(s_sent[(i - 9) % QR], 16 * TOP)
                    act.wait_ge(s_z, i - 8)
                    a.activation(rows[:, (i - 9) % QR, HI:HI + E // 2].bitcast(f16), z[:, (i - 9) % 2, :], ACT.Copy,
                                 scale=XW).then_inc(s_hi, 1)
                if live(i):
                    act.wait_ge(s_Q, i + 1)
                    a.activation(eq[:, i % 2, :], pQ[i % 2], ACT.Exp).then_inc(s_exp, 1)
                if live(i - 1):
                    act.wait_ge(s_QT, i)
                    a.activation(qT[:, (i - 1) % QR, :], pQT[(i - 1) % 2], ACT.Copy).then_inc(s_qT, 1)
                if live(i + 1):
                    act.wait_ge(s_rs1, 3 * ((i + 1) // PER + 1))
                    a.activation(xn[:, (i + 1) % 2, :], xall[:, i + 1, :], ACT.Identity, scale=rs1[:, i + 1:i + 2],
                                 bias=nm1[:, i + 1:i + 2]).then_inc(s_xn, 1)
                if i >= TILES:
                    evacuate_z(i)
                if i <= TILES + 1:
                    normalise(i)
                if live(i):
                    act.wait_ge(s_VU, i + 1)
                    a.activation(th[:, i % 2, :], pVU[i % 2], ACT.Tanh, scale=0.5).then_inc(s_tanh, 1)
                widen(i)
                if i < TILES:
                    evacuate_z(i)
                if live(i + 1):
                    act.wait_ge(s_XT, i + 2)
                    a.activation(xT[:, (i + 1) % 2, :, :].rearrange("p k t -> p (k t)"), pXT[(i + 1) % 2], ACT.Copy)\
                     .then_inc(s_xT, 1)
                for n in chunks_of(i):
                    chunk_high(n)

            act.wait_ge(s_warm, 1)
            a.activation(warm[:], neghalf[:, 0:1], ACT.Silu).then_inc(s_warm, 1)
            act.wait_ge(s_padoff, 1)
            for e in range(EXPERTS // 2):
                off = act.value_load(padoff_i[0:1, e:e + 1], min_val=0, max_val=SPARE - P)
                act.dma_start(sent[bass.ds(off, P), :], padrows[:, :]).then_inc(s_padA, 16)

            def step(j, par):
                act.wait_ge(s_H0, j + 1)
                a.activation(sil[par], pH0[par], ACT.Silu, scale=1.0 / (XW * WW)).then_inc(s_sil, 1)
                act.wait_ge(s_IT, j + 1)
                a.activation(ih[par].rearrange("p k t -> p (k t)"), pIT, ACT.Copy).then_inc(s_ih, 1)
            step(0, 0)
            with act.Fori(0, (BLOCKS - 3) // SL) as k:
                for r in range(SL):
                    step(SL * k + 1 + r, (1 + r) % 2)
            for j in range(BLOCKS - 2, BLOCKS):
                step(j, j % 2)

        @block.vector
        def _(dve):
            v = nc.vector

            def ln1_stats(grp):
                dve.wait_ge(s_xin[grp], 16)
                for i in range(PER * grp, PER * grp + PER):
                    v.bn_stats(st1[:, i, :], xall[:, i, :]).then_inc(s_st1, 1)
                for i in range(PER * grp, PER * grp + PER):
                    dve.wait_ge(s_st1, i + 1)
                    v.bn_aggr(mv1[:, i, :], st1[:, i, :]).then_inc(s_mv1, 1)
                dve.wait_ge(s_mv1, PER * grp + PER)
                v.tensor_scalar(ve1[:, PER * grp:PER * grp + PER], mv1[:, PER * grp:PER * grp + PER, 1], EPS, None,
                                ALU.add).then_inc(s_ve1, 1)
            ln1_stats(0)
            dve.wait_ge(s_brow, 64)
            v.tensor_copy(bparts[:, 0, :], bcol[:]).then_inc(s_bsplit, 1)
            dve.wait_ge(s_bsplit, 1)
            v.tensor_tensor(brest[:], bcol[:], bparts[:, 0, :], ALU.subtract).then_inc(s_bsplit, 1)
            dve.wait_ge(s_bsplit, 2)
            v.tensor_copy(bparts[:, 1, :], brest[:]).then_inc(s_bsplit, 1)
            dve.wait_ge(s_bsplit, 3)
            v.tensor_tensor(bcol[:], brest[:], bparts[:, 1, :], ALU.subtract).then_inc(s_bsplit, 1)
            dve.wait_ge(s_bsplit, 4)
            v.tensor_copy(bparts[:, 2, :], bcol[:]).then_inc(s_bsplit, 1)
            v.memset(ones16[:], 1.0).then_inc(s_fill, 1)
            v.memset(sofar[:], 0.0).then_inc(s_fill, 1)
            v.memset(oneE[:], 1.0).then_inc(s_fill, 1)
            dve.wait_ge(s_fill, 3)

            def chunk_low(n):
                dve.wait_ge(s_whi, n + 1)
                at_ = slice(n % NCH * CH, n % NCH * CH + CH)
                v.scalar_tensor_tensor(w_lo[:, n // NCH, at_], stage[:, n % NCH, :], WW, w_hi[:, n // NCH, at_],
                                       ALU.mult, ALU.subtract).then_inc(s_wlo, 1)

            chain = [0]

            def link(ins):
                chain[0] += 1
                ins.then_inc(s_route, 1)
                dve.wait_ge(s_route, chain[0])

            def wide(small, nt):
                return small.unsqueeze(2).to_broadcast([P, nt, EXPERTS])

            def route_best(n):
                nt = GROUP[n][1]
                w = slice(0, nt)
                link(v.tensor_reduce(m0[:, w], lg[:, w], AX.X, ALU.max))
                link(v.tensor_tensor(same[:, w], lg[:, w], wide(m0[:, w], nt), ALU.is_equal))
                link(v.tensor_tensor(first[:, w], same[:, w], desc[:, w], ALU.mult))
                link(v.tensor_reduce(k0[:, w], first[:, w], AX.X, ALU.max))
                v.tensor_tensor(oh0[:, w], first[:, w], wide(k0[:, w], nt), ALU.is_equal).then_inc(s_oh, 1)

            def route_second(n):
                nt = GROUP[n][1]
                w = slice(0, nt)
                dve.wait_ge(s_oh, 2 * n + 1)
                link(v.scalar_tensor_tensor(lg2[:, w], oh0[:, w], -3.0e38, lg[:, w], ALU.mult, ALU.add))
                link(v.tensor_reduce(m1[:, w], lg2[:, w], AX.X, ALU.max))
                v.tensor_tensor(dm[:, w], m1[:, w], m0[:, w], ALU.subtract).then_inc(s_dm, 1)
                link(v.tensor_tensor(same[:, w], lg2[:, w], wide(m1[:, w], nt), ALU.is_equal))
                link(v.tensor_tensor(first[:, w], same[:, w], desc[:, w], ALU.mult))
                link(v.tensor_reduce(k0[:, w], first[:, w], AX.X, ALU.max))
                v.tensor_tensor(oh1[:, w], first[:, w], wide(k0[:, w], nt), ALU.is_equal).then_inc(s_oh, 1)

            def route_count(n):
                nt = GROUP[n][1]
                dve.wait_ge(s_oh, 2 * n + 2)
                v.tensor_tensor(chosen[:, n % 2, 0:nt], oh0[:, 0:nt], oh1[:, 0:nt], ALU.add).then_inc(s_chosen, 1)
                dve.wait_ge(s_chosen, n + 1)
                with nc.allow_low_precision("counts up to 16 are exact in bf16"):
                    link(v.tensor_reduce(inside[:], chosen[:, n % 2, 0:nt].rearrange("p t e -> p e t"), AX.X, ALU.add))
                v.tensor_tensor(sofar[:, 1 - n % 2], sofar[:, n % 2], inside[:], ALU.add).then_inc(s_sofar, 1)

            def route_rows(n):
                t0, nt = GROUP[n]
                w = slice(0, nt)
                r = slice(t0 % QR, t0 % QR + nt)
                if n >= 3:
                    for t in range(GROUP[n - 3][0], sum(GROUP[n - 3])):
                        dve.wait_ge(s_sent[t % QR], 16 * TOP * (t // QR + 1))
                dve.wait_ge(s_ex, n + 1)
                link(v.tensor_scalar(dm[:, w], ex[:, w], 1.0, None, ALU.add))
                link(v.reciprocal(p0[:, w], dm[:, w]))
                dve.wait_ge(s_R, n + 1)
                v.tensor_tensor(place[:, w], pR[n][:, 0:nt * EXPERTS].rearrange("p (t e) -> p t e", e=EXPERTS),
                                region0[:, w], ALU.add).then_inc(s_place, 1)
                v.tensor_tensor(c0[:, w], oh0[:, w], wide(p0[:, w], nt), ALU.mult)
                link(v.tensor_tensor(p1[:, w], ex[:, w], p0[:, w], ALU.mult))
                dve.wait_ge(s_place, n + 1)
                v.tensor_tensor(h0[:, w], place[:, w], oh0[:, w], ALU.mult)
                v.tensor_tensor(h1[:, w], place[:, w], oh1[:, w], ALU.mult)
                link(v.tensor_tensor(c1[:, w], oh1[:, w], wide(p1[:, w], nt), ALU.mult))
                v.tensor_reduce(slots[:, 0, w], h0[:, w], AX.X, ALU.add)
                v.tensor_tensor(rows[:, r, COMB:COMB + EXPERTS], c0[:, w], c1[:, w], ALU.add)
                v.tensor_copy(rows[:, r, TOK].bitcast(i32), tokno[:, t0:t0 + nt])
                link(v.tensor_reduce(slots[:, 1, w], h1[:, w], AX.X, ALU.add))
                v.tensor_copy(slots_i[:, n % 3, :, w], slots[:, :, w]).then_inc(s_slots, 1)

            ln1_stats(1)
            for n in chunks_of(FIRST_STEP):
                chunk_low(n)

            def take_stats(i):
                for j in stats_of(i):
                    dve.wait_ge(s_O, j + 1)
                    v.bn_stats(st2[:, j % QR, :], pO[j]).then_inc(s_st2, 1)
                for j in stats_of(i):
                    dve.wait_ge(s_st2, j + 1)
                    v.bn_aggr(mv2[:, j % QR, :], st2[:, j % QR, :]).then_inc(s_mv2, 1)

            def times_u(i):
                if live(i - 6):
                    dve.wait_ge(s_onT, KT * (i - 5))
                    v.tensor_tensor(yT[:, i % 2, :], onT[:], uring[:, (i - 6) % 8, :], ALU.mult).then_inc(s_y, 1)

            def cut_kv(i):
                if i % PER == 0 and 0 < i <= TILES:
                    dve.wait_ge(s_KV, i)
                    v.tensor_tensor(kv[:, (i // PER - 1) % 2, :], pKV, headmask[:], ALU.mult).then_inc(s_kv, 1)

            for i in range(0, STEPS):
                best = routed(i, 10)
                places = routed(i, 11)
                if i == 1:
                    dve.wait_ge(s_const, CONST_STEPS)
                    dve.wait_ge(s_gb, 16 * 2 * KT)
                    v.tensor_scalar(gamma[:], gamma[:], 0.5, None, ALU.mult).then_inc(s_gbh, 1)
                    v.tensor_scalar(beta[:], beta[:], 0.5, None, ALU.mult).then_inc(s_gbh, 1)
                if live(i - 10):
                    dve.wait_ge(s_G, i - 9)
                    t0 = GROUP[group_of(i - 10)][0]
                    v.tensor_copy(lg[:, i - 10 - t0, :], pG).then_inc(s_lg, 1)
                if live(i - 8):
                    if i - 8 >= PER:
                        dve.wait_ge(s_store[(i - 8) % PER], 16 * ((i - 8) // PER))
                    dve.wait_ge(s_W, i - 7)
                    if routed(i - 1, 11) == 0:
                        dve.wait_ge(s_R, 1)
                    v.tensor_tensor(x2[:, (i - 8) % PER, :], pW, xall[:, i - 8, :], ALU.add).then_inc(s_x2, 1)
                if i - 1 <= TILES:
                    take_stats(i - 1)
                if live(i - 8):
                    dve.wait_ge(s_x2, i - 7)
                    v.bn_stats(st3[:, i % 2, :], x2[:, (i - 8) % PER, :]).then_inc(s_st3, 1)
                if live(i - 9):
                    dve.wait_ge(s_hi, i - 8)
                    r = (i - 9) % QR
                    v.scalar_tensor_tensor(rows[:, r, LO:LO + E // 2].bitcast(f16), z[:, (i - 9) % 2, :], XW,
                                           rows[:, r, HI:HI + E // 2].bitcast(f16), ALU.mult, ALU.subtract).then_inc(s_lo, 1)
                if live(i - 8):
                    dve.wait_ge(s_st3, i - 7)
                    v.bn_aggr(mv3[:, i % 2, :], st3[:, i % 2, :]).then_inc(s_mv3, 1)
                if live(i):
                    dve.wait_ge(s_exp, i + 1)
                    v.tensor_scalar(eq[:, i % 2, :], eq[:, i % 2, :], 1.0, -1.0, ALU.min, ALU.add).then_inc(s_em1, 1)
                if live(i):
                    dve.wait_ge(s_em1, i + 1)
                    v.scalar_tensor_tensor(q[:, i % 2, :], pQ[i % 2], 0.0, eq[:, i % 2, :], ALU.max, ALU.add).then_inc(s_q, 1)
                if i > TILES:
                    times_u(i)
                if i == TILES:
                    cut_kv(i)
                if live(i - 8):
                    dve.wait_ge(s_rs3, i - 7)
                    v.tensor_scalar(z[:, i % 2, :], x2[:, (i - 8) % PER, :], mv3[:, i % 2, 0:1], rs3[:, i % 2:i % 2 + 1],
                                    ALU.subtract, ALU.mult).then_inc(s_z, 1)
                if i == TILES + 1:
                    take_stats(i)
                if best is not None:
                    dve.wait_ge(s_lg, i - 9)
                    route_best(best)
                if best is not None:
                    route_second(best)
                if best is not None:
                    route_count(best)
                for n in chunks_of(i - 1) if i > 0 else []:
                    chunk_low(n)
                if places == len(GROUP) - 1:
                    dve.wait_ge(s_C, 1)
                    link(v.tensor_copy(count[:], pC))
                    v.tensor_tensor(padoff_i[:], count[:], region0[:, 0, :], ALU.add).then_inc(s_padoff, 1)
                if places is not None and places > 0:
                    route_rows(places)
                if i in (1, 3):
                    ln1_stats((i + 3) // 2)
                if live(i):
                    dve.wait_ge(s_tanh, i + 1)
                    v.scalar_tensor_tensor(vv[:, i % 2, :], th[:, i % 2, 0:E], 1.0, pVU[i % 2][:, 0:E], ALU.add, ALU.mult)\
                     .then_inc(s_v, 1)
                    v.scalar_tensor_tensor(uring[:, i % 8, :], th[:, i % 2, E:2 * E], 1.0, pVU[i % 2][:, E:2 * E], ALU.add,
                                           ALU.mult).then_inc(s_u, 1)
                if i <= TILES:
                    times_u(i)
                if places == 0:
                    route_rows(places)
                if i < TILES:
                    cut_kv(i)

            BE = [P, BLOCKS, EXPERTS]
            link(v.tensor_tensor(over, count[:].unsqueeze(2).to_broadcast([P, EXPERTS, TILES]), thresholds[:], ALU.is_gt))
            link(v.tensor_reduce(nblk[:], over, AX.X, ALU.add))
            link(v.tensor_tensor_scan(ends[:], oneE[:], nblk[:], 0.0, ALU.mult, ALU.add))
            link(v.tensor_tensor(past, ends[:].unsqueeze(1).to_broadcast(BE), blockno[:], ALU.is_le))
            link(v.tensor_reduce(bexp, past, AX.X, ALU.add))
            link(v.tensor_tensor(past2, past, nblk[:].unsqueeze(1).to_broadcast(BE), ALU.mult))
            link(v.tensor_reduce(bstart, past2, AX.X, ALU.add))
            link(v.scalar_tensor_tensor(boff, bstart, -float(P), block128[:], ALU.mult, ALU.add))
            link(v.scalar_tensor_tensor(boff, bexp, float(REGION), boff, ALU.mult, ALU.add))
            link(v.tensor_scalar(boff_i[:], boff, float(SPARE), None, ALU.min))
            link(v.tensor_scalar(bexp_i[:], bexp, float(EXPERTS - 1), None, ALU.min))
            dve.sem_inc(s_table, 1)

            def rows_turned(j, par):
                dve.wait_ge(s_XB, j + 1)
                v.tensor_copy(xb[par], pXB).then_inc(s_xb, 1)

            def step(j, slot, head, tail):
                par = slot % 2
                dve.wait_ge(s_sil, j + 1)
                dve.wait_ge(s_H1, j + 1)
                v.scalar_tensor_tensor(inter[par], pH1[par], IW / (XW * WW), sil[par], ALU.mult, ALU.mult)\
                 .then_inc(s_inter, 1)
                if not tail:
                    rows_turned(j + 1, 1 - par)
                if not head:
                    weigh(j - 1, (slot - 1) % SL)
                dve.wait_ge(s_ih, j + 1)
                dve.wait_ge(s_IT, j + 1)
                v.tensor_tensor(il[par].rearrange("p k t -> p (k t)"), pIT, ih[par].rearrange("p k t -> p (k t)"),
                                ALU.subtract).then_inc(s_il, 1)

            def weigh(j, slot):
                e = dve.value_load(bexp_i[0:1, bass.ds(j, 1)], min_val=0, max_val=EXPERTS - 1)
                dve.wait_ge(s_Y, j + 1)
                v.tensor_scalar(ys[slot], pY[slot % 2], blk[slot][:, bass.ds(COMB + e, 1)], 1.0 / (IW * WW),
                                ALU.mult, ALU.mult).then_inc(s_ys, 1)
            rows_turned(0, 0)
            step(0, 0, True, False)
            with dve.Fori(0, (BLOCKS - 3) // SL) as k:
                for r in range(SL):
                    step(SL * k + 1 + r, (1 + r) % SL, False, False)
            step(BLOCKS - 2, (BLOCKS - 2) % SL, False, False)
            step(BLOCKS - 1, (BLOCKS - 1) % SL, False, True)
            weigh(BLOCKS - 1, (BLOCKS - 1) % SL)

        @block.tensor
        def _(pe):
            m = nc.tensor
            pe.wait_ge(s_const, 7)

            def turn(dst, src, done):
                for k in range(KT):
                    mm = m.transpose(dst[:, k * P:(k + 1) * P], src[:, k * P:(k + 1) * P], ident[:])
                mm.then_inc(done, 1)

            def project(dst, lhs, w, c0_, n, done):
                m.matmul(dst, ones16[0:3, :], bias3[:, c0_:c0_ + n], start=True, stop=False)
                for k in range(KT):
                    mm = m.matmul(dst, lhs[:, k, :], w[:, k, :], start=False, stop=(k == KT - 1))
                mm.then_inc(done, 1)

            def turn_y(i):
                if live(i - 6):
                    pe.wait_ge(s_on, i - 5)
                    turn(pYT, on[:, i % 2, :], s_YT)

            def q_kv(i):
                for j in stats_of(i):
                    pe.wait_ge(s_kv, j // PER + 1)
                    pe.wait_ge(s_qT, j + 1)
                    if j >= TILES - PER:
                        pe.wait_ge(s_u, TILES)
                        pe.wait_ge(s_q, TILES)
                        pe.wait_ge(s_qT, TILES)
                    elif j >= 1:
                        pe.wait_ge(s_onT, KT * j)
                    for k in range(KT):
                        kc = slice(k * P, (k + 1) * P)
                        mm = m.matmul(pO[j][:, kc], qT[:, j % QR, kc], kv[:, j // PER % 2, kc], start=True, stop=True)
                    mm.then_inc(s_O, 1)

            def turn_z(i):
                if live(i - 9):
                    pe.wait_ge(s_z, i - 8)
                    if live(i - 10):
                        pe.wait_ge(s_lg, i - 9)
                    turn(pZT, z[:, (i - 9) % 2, :], s_ZT)

            def add_kv(i):
                if live(i - 1):
                    j = i - 1
                    pe.wait_ge(s_v, i)
                    if j % PER == 0 and j > 0:
                        pe.wait_ge(s_kv, j // PER)
                    for k in range(KT):
                        kc = slice(k * P, (k + 1) * P)
                        mm = m.matmul(pKV[:, kc], q[:, j % 2, kc], vv[:, j % 2, kc], start=(j % PER == 0 and k == 0),
                                      stop=(j % PER == PER - 1), skip_group_check=True)
                    mm.then_inc(s_KV, 1)

            def wo_product(i):
                if live(i - 7):
                    if i == 7:
                        pe.wait_ge(s_wB, 32)
                    pe.wait_ge(s_y, i - 6)
                    if live(i - 8):
                        pe.wait_ge(s_x2, i - 7)
                    if routed(i - 1, 11) == 0:
                        pe.wait_ge(s_place, 1)
                    project(pW, yT[:, (i - 7) % 2, :].rearrange("p (k t) -> p k t", t=P), wout, 3 * E, E, s_W)

            def ranks(i):
                n = routed(i, 11)
                if n == 0:
                    pe.wait_ge(s_const, CONST_STEPS)
                if n is not None:
                    nt = GROUP[n][1]
                    pe.wait_ge(s_chosen, n + 1)
                    if n > 0:
                        pe.wait_ge(s_sofar, n)
                        pe.wait_ge(s_kv, GROUPS)
                        pe.wait_ge(s_place, n)
                    m.matmul(pR[n][:, 0:nt * EXPERTS], before[:], chosen[:, n % 2, 0:nt].rearrange("p t e -> p (t e)"),
                             start=True, stop=False)
                    for d in range(1, nt):
                        m.matmul(pR[n][:, d * EXPERTS:nt * EXPERTS], ones16[:],
                                 chosen[:, n % 2, 0:nt - d].rearrange("p t e -> p (t e)"), start=False, stop=False)
                    for t in range(nt):
                        mm = m.matmul(pR[n][:, t * EXPERTS:(t + 1) * EXPERTS], ones16[:], sofar[:, n % 2],
                                      start=False, stop=(t == nt - 1))
                    mm.then_inc(s_R, 1)
                if n == len(GROUP) - 1:
                    pe.wait_ge(s_sofar, n + 1)
                    m.matmul(pC, ones16[:], sofar[:, len(GROUP) % 2], start=True, stop=True).then_inc(s_C, 1)

            for i in range(FIRST_STEP, STEPS):
                if live(i):
                    pe.wait_ge(s_xT, i + 1)
                    if i == 0:
                        pe.wait_ge(s_wA, 48)
                        pe.wait_ge(s_bias3, 48)
                        pe.wait_ge(s_fill, 1)
                    project(pQ[i % 2], xT[:, i % 2], wcat[:, :, 0:E], 0, E, s_Q)
                if live(i - 1):
                    pe.wait_ge(s_q, i)
                    turn(pQT[(i - 1) % 2], q[:, (i - 1) % 2, :], s_QT)
                if live(i):
                    if i >= 2:
                        pe.wait_ge(s_u, i - 1)
                    project(pVU[i % 2][:, 0:E], xT[:, i % 2], wcat[:, :, E:2 * E], E, E, s_V)
                    for c in range(KT):
                        dst = pVU[i % 2][:, E + c * P:E + (c + 1) * P]
                        c0_ = 2 * E + c * P
                        m.matmul(dst, bias3[:, c0_:c0_ + P], ones16[0:3, :], start=True, stop=False)
                        for k in range(KT):
                            mm = m.matmul(dst, wcat[:, k, c0_:c0_ + P], xT[:, i % 2, k, :], start=False, stop=(k == KT - 1))
                    mm.then_inc(s_VU, 1)
                if i < TILES:
                    turn_y(i)
                    turn_z(i)
                    if live(i + 1):
                        pe.wait_ge(s_xn, i + 2)
                        if live(i - 1):
                            pe.wait_ge(s_qT, i)
                        turn(pXT[(i + 1) % 2], xn[:, (i + 1) % 2, :], s_XT)
                    add_kv(i)
                    wo_product(i)
                    q_kv(i)
                elif i < TILES + 2:
                    add_kv(i)
                    turn_z(i)
                    wo_product(i)
                    turn_y(i)
                    q_kv(i)
                else:
                    ranks(i)
                    turn_y(i)
                    turn_z(i)
                    wo_product(i)
                if i <= TILES:
                    ranks(i)
                if live(i - 9):
                    pe.wait_ge(s_zT, i - 8)
                    for k in range(KT):
                        mm = m.matmul(pG, zT[:, k * P:(k + 1) * P], gatew[:, k, :], start=(k == 0), stop=(k == KT - 1))
                    mm.then_inc(s_G, 1)

            def turn_rows(j, slot, uses):
                pe.wait_ge(s_blk[slot], 16 * uses)
                r16 = blk[slot][:, 0:E].bitcast(f16)
                for k in range(2 * KT):
                    mm = m.transpose(pXB[:, k, :], r16[:, k * P:(k + 1) * P], ident16[:])
                mm.then_inc(s_XB, 1)

            def three(dst, pairs, done):
                last = len(pairs) * 3 - 1
                n = 0
                for hi, lo_, wh, wl in pairs:
                    for l, r in ((hi, wh), (hi, wl), (lo_, wh)):
                        mm = m.matmul(dst, l, r, start=(n == 0), stop=(n == last))
                        n += 1
                mm.then_inc(done, 1)

            def up(j, slot, e):
                par = slot % 2
                pe.wait_ge(s_xb, j + 1)
                for c, dst, done in ((0, pH0[par], s_H0), (1, pH1[par], s_H1)):
                    three(dst, [(xb[par][:, k, :], xb[par][:, KT + k, :],
                                 weights_of(w_hi, e, c * CH + k * MLP, MLP), weights_of(w_lo, e, c * CH + k * MLP, MLP))
                                for k in range(KT)], done)

            def turn_inter(j, slot):
                par = slot % 2
                pe.wait_ge(s_inter, j + 1)
                for k in range(MT):
                    mm = m.transpose(pIT[:, k * P:(k + 1) * P], inter[par][:, k * P:(k + 1) * P], ident[:])
                mm.then_inc(s_IT, 1)

            def down(j, slot, e):
                par = slot % 2
                pe.wait_ge(s_il, j + 1)
                three(pY[par], [(ih[par][:, k, :], il[par][:, k, :], weights_of(w_hi, e, 2 * CH + k * E, E),
                                 weights_of(w_lo, e, 2 * CH + k * E, E)) for k in range(MT)], s_Y)

            def expert_of(j):
                return pe.value_load(bexp_i[0:1, bass.ds(j, 1)], min_val=0, max_val=EXPERTS - 1)

            def step(j, slot, uses, e_last, e, ahead, head=False):
                up(j, slot, e)
                if uses is not None:
                    turn_rows(j + 1, (slot + 1) % SL, uses)
                if not head:
                    down(j - 1, (slot - 1) % SL, expert_of(j - 1) if e_last is None else e_last)
                e_next = expert_of(j + 1) if ahead else None
                turn_inter(j, slot)
                return e_next
            pe.wait_ge(s_table, 1)
            pe.wait_ge(s_wlo, NCH * EXPERTS)
            turn_rows(0, 0, 1)
            step(0, 0, 1, None, expert_of(0), False, head=True)
            with pe.Fori(0, (BLOCKS - 3) // SL) as k:
                e_last, e = None, expert_of(SL * k + 1)
                for r in range(SL):
                    e_last, e = e, step(SL * k + 1 + r, (1 + r) % SL, k + (r + 2) // SL + 1, e_last, e, r < SL - 1)
            e_last, e = None, expert_of(BLOCKS - 2)
            e_last, e = e, step(BLOCKS - 2, (BLOCKS - 2) % SL, (BLOCKS - 1) // SL + 1, e_last, e, True)
            step(BLOCKS - 1, (BLOCKS - 1) % SL, None, e_last, e, False)
            down(BLOCKS - 1, (BLOCKS - 1) % SL, e)


_INS = ['x', 'Wqk', 'bqk', 'Wv', 'bv', 'Wu', 'bu', 'Wo', 'bo', 'ln_g', 'ln_b']
_FFN = ['gate_kernel', 'w0_kernel', 'w1_kernel', 'wo_kernel']


def kernel(**inputs):
    import numpy as _np
    import concourse.bacc as _bacc
    from concourse import mybir as _mybir
    from concourse.bass_utils import run_bass_kernel_spmd as _run

    nc = _bacc.Bacc("TRN2", target_bir_lowering=False, num_devices=1)
    arrays, args = {}, []
    for name in ['L0_attn_' + n for n in _INS] + ['L0_ffn_' + n for n in _FFN]:
        a = _np.ascontiguousarray(inputs[name])
        if name == 'L0_attn_x':
            batch, seq, width = a.shape
            a = a.reshape(batch * seq, width)
        arrays["in_" + name] = a
        args.append(nc.dram_tensor("in_" + name, a.shape, _mybir.dt.from_np(a.dtype), kind="ExternalInput").ap())
    out = nc.dram_tensor("out_0", (batch * seq + 128, width), _mybir.dt.float32, kind="ExternalOutput").ap()
    linear_attention_then_top2_moe(nc, *args, out)
    r = _run(nc, [arrays], core_ids=[0])
    return r.results[0]["out_0"][:batch * seq].reshape(batch, seq, width)
```
